# Optimizing a Trainium2 kernel written in Bass

```python
import numpy as np
import jax
import jax.numpy as jnp

def _softmax(x, axis=-1):
    return jax.nn.softmax(x, axis=axis)
def _gelu(x):
    return jax.nn.gelu(x, approximate=True)
def _silu(x):
    return jax.nn.silu(x)
def _sigmoid(x):
    return jax.nn.sigmoid(x)
def _layernorm(x, axis=-1, eps=1e-5):
    m = jnp.mean(x, axis=axis, keepdims=True)
    v = jnp.var(x, axis=axis, keepdims=True)
    return (x - m) / jnp.sqrt(v + eps)
def _scatter_add(tgt, idx, src, axis=0):
    return tgt.at[idx].add(src)
def _segment_sum(src, seg, n):
    return jax.ops.segment_sum(src, seg, n)

kernel_name = 'mk_conv_attn_hybrid_d2_conv_nhwc128_922dd7'

def setup_inputs(seed: int = 0):
    np.random.seed(seed)
    _w = jnp.asarray
    def _rec_inputs():
        import jax
        import jax.numpy as jnp
        _gk = jax.random.key(seed)
        x = -0.0005153 + 1.001 * jax.random.normal(jax.random.fold_in(_gk, 1), (8, 56, 56, 128), jnp.float32)
        return x
    x = _rec_inputs()
    def _L0_conv_setup():
        import jax, jax.numpy as jnp
        import numpy as np
        KH = KW = 3
        PAD = 1
        DIL = 1
        GROUP = 4
        OFFSET_SCALE = 1.0
        P = KH * KW

        def bilinear_sample(img, iy, ix, H, W):
            x0 = jnp.floor(ix)
            y0 = jnp.floor(iy)
            wx1 = ix - x0
            wy1 = iy - y0

            def corner(yf, xf, wgt):
                valid = (yf >= 0) & (yf < H) & (xf >= 0) & (xf < W)
                idx = jnp.clip(yf, 0, H - 1).astype(jnp.int32) * W + jnp.clip(xf, 0, W - 1).astype(jnp.int32)
                v = jax.vmap(lambda im, i: im[i])(img, idx)
                return v * (wgt * valid)[..., None]
            return corner(y0, x0, (1 - wy1) * (1 - wx1)) + corner(y0, x0 + 1, (1 - wy1) * wx1) + corner(y0 + 1, x0, wy1 * (1 - wx1)) + corner(y0 + 1, x0 + 1, wy1 * wx1)

        def dcn_core(x_proj, offset, mask_sm):
            N, H, W, C = x_proj.shape
            Hin, Win = (H + 2 * PAD, W + 2 * PAD)
            Cg = C // GROUP
            pad = jnp.pad(x_proj, ((0, 0), (PAD, PAD), (PAD, PAD), (0, 0)))
            img = pad.reshape(N, Hin, Win, GROUP, Cg).transpose(0, 3, 1, 2, 4).reshape(N * GROUP, Hin * Win, Cg)
            ref_x = (jnp.arange(W, dtype=jnp.float32) + DIL * (KW - 1) // 2 + 0.5) / Win
            ref_y = (jnp.arange(H, dtype=jnp.float32) + DIL * (KH - 1) // 2 + 0.5) / Hin
            gx = jnp.arange(KW, dtype=jnp.float32) * DIL - DIL * (KW - 1) // 2
            gy = jnp.arange(KH, dtype=jnp.float32) * DIL - DIL * (KH - 1) // 2
            gxx, gyy = jnp.meshgrid(gx, gy, indexing='ij')
            gpx = (gxx / Win).reshape(P)
            gpy = (gyy / Hin).reshape(P)
            loc_x = ref_x[None, None, :, None, None] + gpx[None, None, None, None, :] * OFFSET_SCALE + offset[..., 0] * (OFFSET_SCALE / Win)
            loc_y = ref_y[None, :, None, None, None] + gpy[None, None, None, None, :] * OFFSET_SCALE + offset[..., 1] * (OFFSET_SCALE / Hin)
            ix = (loc_x * Win - 0.5).transpose(0, 3, 1, 2, 4).reshape(N * GROUP, H * W * P)
            iy = (loc_y * Hin - 0.5).transpose(0, 3, 1, 2, 4).reshape(N * GROUP, H * W * P)
            samp = bilinear_sample(img, iy, ix, Hin, Win)
            samp = samp.reshape(N, GROUP, H, W, P, Cg)
            return jnp.einsum('nghwpc,nhwgp->nhwgc', samp, mask_sm).reshape(N, H, W, C)

        def layer_norm(z, g, b, eps=1e-05):
            m = z.mean(-1, keepdims=True)
            v = ((z - m) ** 2).mean(-1, keepdims=True)
            return (z - m) / jnp.sqrt(v + eps) * g + b
        key = jax.random.key(seed)
        ks = jax.random.split(key, 12)
        N, H, W, C, G, R = (8, 56, 56, 128, GROUP, 4)

        def w(k, shp, s=0.02):
            return jax.random.normal(k, shp, jnp.float32) * s
        return dict(x=jax.random.normal(ks[0], (N, H, W, C), jnp.float32), w_in=w(ks[1], (C, C)), b_in=jnp.zeros((C,), jnp.float32), dw_w=w(ks[2], (C, 1, KH, KW)), dw_b=jnp.zeros((C,), jnp.float32), bn_g=jnp.ones((C,), jnp.float32), bn_b=jnp.zeros((C,), jnp.float32), bn_m=w(ks[3], (C,), 0.1), bn_v=jax.random.uniform(ks[4], (C,), jnp.float32, 0.5, 1.5), w_off=w(ks[5], (C, G * P * 2)), b_off=jnp.zeros((G * P * 2,), jnp.float32), w_msk=w(ks[6], (C, G * P)), b_msk=jnp.zeros((G * P,), jnp.float32), w_out=w(ks[7], (C, C)), b_out=jnp.zeros((C,), jnp.float32), ln1_g=jnp.ones((C,), jnp.float32), ln1_b=jnp.zeros((C,), jnp.float32), w_fc1=w(ks[8], (C, R * C)), b_fc1=jnp.zeros((R * C,), jnp.float32), w_fc2=w(ks[9], (R * C, C)), b_fc2=jnp.zeros((C,), jnp.float32), ln2_g=jnp.ones((C,), jnp.float32), ln2_b=jnp.zeros((C,), jnp.float32), gamma1=jnp.ones((C,), jnp.float32), gamma2=jnp.ones((C,), jnp.float32))
    _L0_conv_all = _L0_conv_setup()
    _L0_conv_in = {k: v for k, v in _L0_conv_all.items() if k in ('w_in', 'b_in', 'dw_w', 'dw_b', 'bn_g', 'bn_b', 'bn_m', 'bn_v', 'w_off', 'b_off', 'w_msk', 'b_msk', 'w_out', 'b_out', 'ln1_g', 'ln1_b', 'w_fc1', 'b_fc1', 'w_fc2', 'b_fc2', 'ln2_g', 'ln2_b', 'gamma1', 'gamma2', )}
    del _L0_conv_all

    def _L1_attn_setup():
        import jax, jax.numpy as jnp
        import numpy as np
        key = jax.random.key(seed)
        seq = jax.random.normal(key, (32, 2048, 128), dtype=jnp.float32)
        return {'seq': seq}
    _L1_attn_all = _L1_attn_setup()
    _L1_attn_in = {k: v for k, v in _L1_attn_all.items() if k in ()}
    del _L1_attn_all

    def _L1_ffn_setup():
        import jax, jax.numpy as jnp
        import numpy as np
        B, S, D, E, H, O, K = (512, 2048, 128, 64, 512, 128, 8)
        key = jax.random.key(seed)
        k0, k1, k2, k3 = jax.random.split(key, 4)
        x = jax.random.normal(k0, (B, S, D), dtype=jnp.float32)
        gate_w = jax.random.normal(k1, (E, D), dtype=jnp.float32) * (1.0 / np.sqrt(D))
        gate_b = jnp.zeros((E,), dtype=jnp.float32)
        weight1 = jax.random.uniform(k2, (E, D + 1, H), dtype=jnp.float32, minval=-1.0, maxval=1.0) * (1.0 / np.sqrt(D + 1))
        weight2 = jax.random.uniform(k3, (E, H + 1, O), dtype=jnp.float32, minval=-1.0, maxval=1.0) * (1.0 / np.sqrt(H + 1))
        return {'x': x, 'gate_w': gate_w, 'gate_b': gate_b, 'weight1': weight1, 'weight2': weight2}
    _L1_ffn_all = _L1_ffn_setup()
    _L1_ffn_in = {k: v for k, v in _L1_ffn_all.items() if k in ('gate_w', 'gate_b', 'weight1', 'weight2', )}
    del _L1_ffn_all

    return {
        "x": x,
        "L0_conv_w_in": _L0_conv_in["w_in"],
        "L0_conv_b_in": _L0_conv_in["b_in"],
        "L0_conv_dw_w": _L0_conv_in["dw_w"],
        "L0_conv_dw_b": _L0_conv_in["dw_b"],
        "L0_conv_bn_g": _L0_conv_in["bn_g"],
        "L0_conv_bn_b": _L0_conv_in["bn_b"],
        "L0_conv_bn_m": _L0_conv_in["bn_m"],
        "L0_conv_bn_v": _L0_conv_in["bn_v"],
        "L0_conv_w_off": _L0_conv_in["w_off"],
        "L0_conv_b_off": _L0_conv_in["b_off"],
        "L0_conv_w_msk": _L0_conv_in["w_msk"],
        "L0_conv_b_msk": _L0_conv_in["b_msk"],
        "L0_conv_w_out": _L0_conv_in["w_out"],
        "L0_conv_b_out": _L0_conv_in["b_out"],
        "L0_conv_ln1_g": _L0_conv_in["ln1_g"],
        "L0_conv_ln1_b": _L0_conv_in["ln1_b"],
        "L0_conv_w_fc1": _L0_conv_in["w_fc1"],
        "L0_conv_b_fc1": _L0_conv_in["b_fc1"],
        "L0_conv_w_fc2": _L0_conv_in["w_fc2"],
        "L0_conv_b_fc2": _L0_conv_in["b_fc2"],
        "L0_conv_ln2_g": _L0_conv_in["ln2_g"],
        "L0_conv_ln2_b": _L0_conv_in["ln2_b"],
        "L0_conv_gamma1": _L0_conv_in["gamma1"],
        "L0_conv_gamma2": _L0_conv_in["gamma2"],
        "L1_ffn_gate_w": _L1_ffn_in["gate_w"],
        "L1_ffn_gate_b": _L1_ffn_in["gate_b"],
        "L1_ffn_weight1": _L1_ffn_in["weight1"],
        "L1_ffn_weight2": _L1_ffn_in["weight2"],
    }

def reference(x, L0_conv_w_in, L0_conv_b_in, L0_conv_dw_w, L0_conv_dw_b, L0_conv_bn_g, L0_conv_bn_b, L0_conv_bn_m, L0_conv_bn_v, L0_conv_w_off, L0_conv_b_off, L0_conv_w_msk, L0_conv_b_msk, L0_conv_w_out, L0_conv_b_out, L0_conv_ln1_g, L0_conv_ln1_b, L0_conv_w_fc1, L0_conv_b_fc1, L0_conv_w_fc2, L0_conv_b_fc2, L0_conv_ln2_g, L0_conv_ln2_b, L0_conv_gamma1, L0_conv_gamma2, L1_ffn_gate_w, L1_ffn_gate_b, L1_ffn_weight1, L1_ffn_weight2):
    import jax
    import jax.numpy as jnp
    def _L0_conv_ref(x, w_in, b_in, dw_w, dw_b, bn_g, bn_b, bn_m, bn_v, w_off, b_off, w_msk, b_msk, w_out, b_out, ln1_g, ln1_b, w_fc1, b_fc1, w_fc2, b_fc2, ln2_g, ln2_b, gamma1, gamma2):
        import jax, jax.numpy as jnp
        import numpy as np
        KH = KW = 3
        PAD = 1
        DIL = 1
        GROUP = 4
        OFFSET_SCALE = 1.0
        P = KH * KW

        def bilinear_sample(img, iy, ix, H, W):
            x0 = jnp.floor(ix)
            y0 = jnp.floor(iy)
            wx1 = ix - x0
            wy1 = iy - y0

            def corner(yf, xf, wgt):
                valid = (yf >= 0) & (yf < H) & (xf >= 0) & (xf < W)
                idx = jnp.clip(yf, 0, H - 1).astype(jnp.int32) * W + jnp.clip(xf, 0, W - 1).astype(jnp.int32)
                v = jax.vmap(lambda im, i: im[i])(img, idx)
                return v * (wgt * valid)[..., None]
            return corner(y0, x0, (1 - wy1) * (1 - wx1)) + corner(y0, x0 + 1, (1 - wy1) * wx1) + corner(y0 + 1, x0, wy1 * (1 - wx1)) + corner(y0 + 1, x0 + 1, wy1 * wx1)

        def dcn_core(x_proj, offset, mask_sm):
            N, H, W, C = x_proj.shape
            Hin, Win = (H + 2 * PAD, W + 2 * PAD)
            Cg = C // GROUP
            pad = jnp.pad(x_proj, ((0, 0), (PAD, PAD), (PAD, PAD), (0, 0)))
            img = pad.reshape(N, Hin, Win, GROUP, Cg).transpose(0, 3, 1, 2, 4).reshape(N * GROUP, Hin * Win, Cg)
            ref_x = (jnp.arange(W, dtype=jnp.float32) + DIL * (KW - 1) // 2 + 0.5) / Win
            ref_y = (jnp.arange(H, dtype=jnp.float32) + DIL * (KH - 1) // 2 + 0.5) / Hin
            gx = jnp.arange(KW, dtype=jnp.float32) * DIL - DIL * (KW - 1) // 2
            gy = jnp.arange(KH, dtype=jnp.float32) * DIL - DIL * (KH - 1) // 2
            gxx, gyy = jnp.meshgrid(gx, gy, indexing='ij')
            gpx = (gxx / Win).reshape(P)
            gpy = (gyy / Hin).reshape(P)
            loc_x = ref_x[None, None, :, None, None] + gpx[None, None, None, None, :] * OFFSET_SCALE + offset[..., 0] * (OFFSET_SCALE / Win)
            loc_y = ref_y[None, :, None, None, None] + gpy[None, None, None, None, :] * OFFSET_SCALE + offset[..., 1] * (OFFSET_SCALE / Hin)
            ix = (loc_x * Win - 0.5).transpose(0, 3, 1, 2, 4).reshape(N * GROUP, H * W * P)
            iy = (loc_y * Hin - 0.5).transpose(0, 3, 1, 2, 4).reshape(N * GROUP, H * W * P)
            samp = bilinear_sample(img, iy, ix, Hin, Win)
            samp = samp.reshape(N, GROUP, H, W, P, Cg)
            return jnp.einsum('nghwpc,nhwgp->nhwgc', samp, mask_sm).reshape(N, H, W, C)

        def layer_norm(z, g, b, eps=1e-05):
            m = z.mean(-1, keepdims=True)
            v = ((z - m) ** 2).mean(-1, keepdims=True)
            return (z - m) / jnp.sqrt(v + eps) * g + b
        N, H, W, C = x.shape
        xp = x @ w_in + b_in
        h = x.transpose(0, 3, 1, 2)
        h = jax.lax.conv_general_dilated(h, dw_w, (1, 1), ((PAD, PAD), (PAD, PAD)), feature_group_count=C, dimension_numbers=('NCHW', 'OIHW', 'NCHW')) + dw_b[None, :, None, None]
        h = (h - bn_m[None, :, None, None]) * (bn_g / jnp.sqrt(bn_v + 1e-05))[None, :, None, None] + bn_b[None, :, None, None]
        h = jax.nn.gelu(h.transpose(0, 2, 3, 1), approximate=False)
        offset = (h @ w_off + b_off).reshape(N, H, W, GROUP, P, 2)
        mask = jax.nn.softmax((h @ w_msk + b_msk).reshape(N, H, W, GROUP, P), axis=-1)
        y = dcn_core(xp, offset, mask) @ w_out + b_out
        x = x + gamma1 * layer_norm(y, ln1_g, ln1_b)
        m = jax.nn.gelu(x @ w_fc1 + b_fc1, approximate=False) @ w_fc2 + b_fc2
        x = x + gamma2 * layer_norm(m, ln2_g, ln2_b)
        return x

    def _L1_attn_ref(seq):
        import jax, jax.numpy as jnp
        import numpy as np
        attn = jnp.einsum('blc,bmc->blm', seq, seq)
        attn = jax.nn.softmax(attn, axis=2)
        out = jnp.einsum('blm,bmc->blc', attn, seq)
        return out

    def _L1_ffn_ref(x, gate_w, gate_b, weight1, weight2):
        import jax, jax.numpy as jnp
        import numpy as np
        B, S, D, E, H, O, K = (512, 2048, 128, 64, 512, 128, 8)
        Bn, Sn, Dn = x.shape
        logits = jnp.einsum('bsd,ed->bse', x, gate_w) + gate_b
        probs = jax.nn.softmax(logits, axis=1)
        vals, idx = jax.lax.top_k(probs.transpose(0, 2, 1), K)
        topv = vals.transpose(0, 2, 1)
        topi = idx.transpose(0, 2, 1)
        flat_idx = topi.reshape(Bn, K * E)
        gathered = jnp.take_along_axis(x, flat_idx[:, :, None], axis=1)
        gathered = gathered.reshape(Bn, K, E, Dn)
        pooled = jnp.einsum('bked,bke->bed', gathered, topv)
        ones = jnp.ones((E, Bn, 1), dtype=x.dtype)
        h = jnp.concatenate([pooled.transpose(1, 0, 2), ones], axis=-1)
        h = jax.nn.gelu(jnp.einsum('ebd,edh->ebh', h, weight1), approximate=False)
        h = jnp.concatenate([h, ones], axis=-1)
        out = jnp.einsum('ebh,eho->ebo', h, weight2)
        out = out.transpose(1, 0, 2)
        weighted = jnp.einsum('beo,bke->bkeo', out, topv).reshape(Bn, K * E, O)
        outputs = jnp.zeros((Bn, Sn, O), dtype=x.dtype)
        outputs = outputs.at[jnp.arange(Bn)[:, None], flat_idx].add(weighted)
        return outputs

    def _gn(v, G=32, eps=1e-5):
        B_, H_, W_, C_ = v.shape
        g = v.reshape(B_, H_, W_, G, C_ // G)
        m = jnp.mean(g, axis=(1, 2, 4), keepdims=True)
        s = jnp.var(g, axis=(1, 2, 4), keepdims=True)
        return ((g - m) / jnp.sqrt(s + eps)).reshape(v.shape)

    def _ln_c(v, eps=1e-6):
        m = jnp.mean(v, axis=-1, keepdims=True)
        s = jnp.var(v, axis=-1, keepdims=True)
        return (v - m) / jnp.sqrt(s + eps)

    def _ln_t(v, eps=1e-5):
        m = jnp.mean(v, axis=-1, keepdims=True)
        s = jnp.var(v, axis=-1, keepdims=True)
        return (v - m) / jnp.sqrt(s + eps)

    def _to_tokens(v):
        B_, H_, W_, C_ = v.shape
        return v.reshape(B_, H_ * W_, C_)
    def _from_tokens(t, like):
        return t.reshape(like.shape)

    x = _L0_conv_ref(x, L0_conv_w_in, L0_conv_b_in, L0_conv_dw_w, L0_conv_dw_b, L0_conv_bn_g, L0_conv_bn_b, L0_conv_bn_m, L0_conv_bn_v, L0_conv_w_off, L0_conv_b_off, L0_conv_w_msk, L0_conv_b_msk, L0_conv_w_out, L0_conv_b_out, L0_conv_ln1_g, L0_conv_ln1_b, L0_conv_w_fc1, L0_conv_b_fc1, L0_conv_w_fc2, L0_conv_b_fc2, L0_conv_ln2_g, L0_conv_ln2_b, L0_conv_gamma1, L0_conv_gamma2)
    t = _to_tokens(x)
    t = t + _L1_attn_ref(_ln_t(t))
    t = t + _L1_ffn_ref(_ln_t(t), L1_ffn_gate_w, L1_ffn_gate_b, L1_ffn_weight1, L1_ffn_weight2)
    x = _from_tokens(t, x)
    return x


_drawn_inputs = setup_inputs


def setup_inputs(seed=0):
    import zlib

    import numpy as np

    out = dict(_drawn_inputs(seed))
    spreads = {'L0_conv_b_in': (0.0, 0.1),
     'L0_conv_dw_b': (0.0, 0.8),
     'L0_conv_bn_g': (1.0, 0.6),
     'L0_conv_bn_b': (0.0, 0.8),
     'L0_conv_b_off': (0.0, 0.492),
     'L0_conv_b_msk': (0.0, 0.8),
     'L0_conv_b_out': (0.0, 0.1),
     'L0_conv_ln1_g': (1.0, 0.2),
     'L0_conv_ln1_b': (0.0, 0.1),
     'L0_conv_b_fc1': (0.0, 0.1),
     'L0_conv_b_fc2': (0.0, 0.1),
     'L0_conv_ln2_g': (1.0, 0.2),
     'L0_conv_ln2_b': (0.0, 0.1),
     'L0_conv_gamma1': (1.0, 0.2),
     'L0_conv_gamma2': (1.0, 0.2),
     'L1_ffn_gate_b': (0.0, 0.1)}
    factors = {'L0_conv_dw_w': 8.0,
     'L0_conv_bn_m': 8.0,
     'L0_conv_bn_v': 8.0,
     'L0_conv_w_off': 8.0,
     'L0_conv_w_msk': 8.0,
     'L1_ffn_gate_w': 8.0,
     'L1_ffn_weight1': 8.0,
     'L1_ffn_weight2': 8.0}
    for name, (base, spread) in spreads.items():
        noise = np.random.default_rng([zlib.crc32(name.encode()), seed]).standard_normal(out[name].shape)
        drawn = base * np.exp(spread * noise) if base else spread * noise
        out[name] = jnp.asarray(drawn.astype(out[name].dtype))
    for name, factor in factors.items():
        out[name] = (out[name] * factor).astype(out[name].dtype)
    return out
```

```python
from contextlib import ExitStack

import numpy as np

import concourse.bass as bass
from concourse import mybir

ALU = mybir.AluOpType
ACT = mybir.ActivationFunctionType
AX = mybir.AxisListType
F32 = mybir.dt.float32
I32 = mybir.dt.int32

NI, HH, WW, C = 8, 56, 56, 128
GR, PT = 4, 9
CG = C // GR
GP = GR * PT
L = HH * WW
TT = 128
NT = -(-L // TT)
LP = NT * TT
TAIL = L - (NT - 1) * TT
RS = 3
NR = 20
WP = WW + 2
HP = RS * NR
PX, PY = WP - 1, RS * NR
TMAX = WP - 1.0
XR = 6 * WP // 3
NE, FF, EF = 64, 512, 512
KT = 4
NG = -(-NT // KT)
SHIFT = 64.0
EPS = 1e-5
RG = 5
NC_OUT = NT // RG

(M_XB, M_MUL, M_Y, M_YT, M_ST1, M_AG1, M_Z1, M_ZA1, M_X1, M_X1T, M_X1B, M_ST2, M_AG2, M_Z2,
 M_ZA2, M_T, M_ST3, M_AG3, M_RSM, M_ZN, M_V, M_ZT) = range(1, 23)
M_N = 22
P_YT, P_OUT, P_X1T, P_FC1, P_FC2, P_ZT = range(1, 7)
P_N = 6
(F_RC, F_T2, F_ST, F_AG, F_Z2, F_Z2T) = range(1, 7)
F_N = 6
(I_CC, I_MX, I_SUB, I_RI, I_RF, I_GT, I_FL, I_FM, I_FR, I_OM, I_TI, I_IDX, I_SM, I_RC, I_MK, I_WY,
 I_W) = range(1, 18)
I_N = 17
R_MX, R_NM, R_RC, R_P, R_M8, R_MR, R_MP, R_PT = range(1, 9)
R_N = 8


class Step:

    def __init__(self, m, par, u, k):
        self.m, self.par, self.u, self.k = m, par, u, k
        self.n = m * 2 + par
        self.t = u * 2 + k
        self.slot = (par + k) % 2

    def tile(self, ahead=0):
        return self.m * (2 * NT) + self.u * 2 + (NT * (self.par + ahead) + self.k)

    def rows(self, ahead=0):
        return self.m * (2 * NR) + self.u * 2 + (NR * (self.par + ahead) + self.k)

    def half(self):
        return self.m * NT + self.u + (NT * self.par + self.k) // 2


def walk(eng, step, image_end):

    def phase(m, par, A, B, D, final=False):
        if A:
            with eng.Fori(0, NR // 2) as u:
                for k in range(2):
                    step(Step(m, par, u, k), A, B, D, True, False)
            rest = NR // 2
        else:
            rest = 0
        with eng.Fori(rest, NT // 2) as u:
            for k in range(2):
                step(Step(m, par, u, k), A, B, D, False, False)
        s = Step(m, par, NT // 2, 0)
        step(s, A, B, D, False, True)
        if D:
            image_end(s)

    phase(-1, 1, True, False, False)
    phase(0, 0, True, True, False)
    with eng.Fori(0, NI // 2 - 1) as m:
        phase(m, 1, True, True, True)
        phase(m + 1, 0, True, True, True)
    phase(NI // 2 - 1, 1, False, True, True)
    phase(NI // 2, 0, False, False, True)


def hybrid(nc, xpad, xtok, padmask, coords, w_in, b_in, taps, chan, w_om, place, b_om, w_out, b_out, affine,
           w_fc1, b_fc1, w_fc2, b_fc2, gate_wt, gate_b, w1, w2, keep, out):
    ctx = ExitStack()
    with ctx:
        def sb(name, shape, dt=F32):
            return ctx.enter_context(nc.sbuf_tensor(name, shape, dt))

        def psum(name):
            return ctx.enter_context(nc.psum_tensor(name, [128, 512], F32))

        def sem(name):
            return ctx.enter_context(nc.semaphore(name))

        table = [nc.dram_tensor(f"table{b}", [GR * PX * PY, 4 * CG], F32).ap() for b in range(2)]
        t_dram = nc.dram_tensor("t_dram", [NI * LP, C], F32).ap()
        t2_dram = nc.dram_tensor("t2_dram", [NI * LP, C], F32).ap()
        z2_dram = nc.dram_tensor("z2_dram", [NI * LP, C], F32).ap()
        mp_dram = nc.dram_tensor("mp_dram", [NI * NE, LP], F32).ap()
        table_v = [t.rearrange("(g x y) c -> x g (y c)", g=GR, x=PX) for t in table]

        ident = sb("ident", [128, 128])
        ones = sb("ones", [1, 128])
        nshift = sb("nshift", [128, 1])
        w_in_s = sb("w_in_s", [C, C])
        b_in_s = sb("b_in_s", [1, C])
        taps_s = sb("taps_s", [C, PT])
        chan_s = sb("chan_s", [C, 5])
        bn = sb("bn", [C, 4])
        w_om_s = sb("w_om_s", [C, 4 * GP])
        place_s = sb("place_s", [3, 4 * GP])
        b_om_s = sb("b_om_s", [1, 4 * GP])
        w_out_s = sb("w_out_s", [C, C])
        b_out_s = sb("b_out_s", [1, C])
        aff_s = sb("aff_s", [128, 6, C])
        A1, B1, A2, B2 = (aff_s[:, i, :] for i in (1, 2, 4, 5))
        w_fc1_s = sb("w_fc1_s", [C, FF])
        b_fc1_s = sb("b_fc1_s", [1, FF])
        w_fc2_s = sb("w_fc2_s", [128, FF // 128, C])
        b_fc2_s = sb("b_fc2_s", [1, C])
        gate_w_s = sb("gate_w_s", [C, NE])
        gate_b_s = sb("gate_b_s", [1, NE])
        keep_s = sb("keep_s", [128, NT])

        xrow = sb("xrow", [XR, 2, 3, C])
        prow = sb("prow", [1, 2, 4 * WP])
        xT = sb("xT", [C, 6, WP])
        patch = sb("patch", [PX, GR, RS, 2, 2, CG])
        acc = sb("acc", [C, RS, WW])
        hT = sb("hT", [C, NR * RS * WW])
        co = sb("co", [3, 2, TT])
        hTs = sb("hTs", [C, TT])
        cc = sb("cc", [128, 2 * GP])
        ri = sb("ri", [128, 2 * GP], I32)
        rf = sb("rf", [128, 2 * GP])
        gt = sb("gt", [128, 2 * GP])
        fl = sb("fl", [128, 2 * GP])
        frac = sb("frac", [128, 2 * GP, 2])
        ti = sb("ti", [128, GP])
        sm = sb("sm", [128, 3, GR])
        ex = sb("ex", [128, GP])
        mk = sb("mk", [128, GP])
        wy = sb("wy", [128, GP, 2])
        idx = sb("idx", [128, NT, GP], I32)
        wts = sb("wts", [128, NT, GP, 2, 2])
        idx_now = sb("idx_now", [128, 2, GP], I32)
        gat = sb("gat", [128, 2, GP, 4, CG])
        xt = sb("xt", [128, C])
        xb = sb("xb", [128, C])
        y = sb("y", [128, C])
        yT = sb("yT", [128, TT])
        st = sb("st", [128, 6])
        mv = sb("mv", [128, 2])
        rstd = sb("rstd", [128, 1])
        lnv = sb("lnv", [128, 2])
        eps = sb("eps", [128, 1])
        rstm = sb("rstm", [128, 1])
        z = sb("z", [128, C])
        za = sb("za", [128, C])
        x1 = sb("x1", [128, C])
        x1b = sb("x1b", [128, C])
        x1T = sb("x1T", [128, TT])
        hs = sb("hs", [128, FF])
        tb = sb("tb", [128, C])
        zn = sb("zn", [128, C])
        zT = sb("zT", [C, 2, LP])
        V1 = sb("V1", [128, 2, NT, C + 1])
        E = sb("E", [128, 2, KT * TT])
        tl = sb("tl", [128, C])
        rc = sb("rc", [128, 1])
        t2 = sb("t2", [128, C])
        st2 = sb("st2", [128, 6])
        mv2 = sb("mv2", [128, 2])
        rs2 = sb("rs2", [128, 1])
        z2 = sb("z2", [128, C])
        z2T = sb("z2T", [C, TT])
        probs = sb("probs", [NE, LP])
        picked = sb("picked", [NE, LP])
        rt = sb("rt", [NE, 4])
        top8 = sb("top8", [NE, 8])
        zc = sb("zc", [128, 2, RG, C])
        mpT = sb("mpT", [128, RG, NE])
        pooled = sb("pooled", [C, NI, NE])
        b1_s = sb("b1_s", [NE, EF])
        b2_s = sb("b2_s", [NE, C])
        eh = sb("eh", [128, EF // 128, NI])

        ps_s = [psum("ps_s0"), psum("ps_s1")]
        ps_o = psum("ps_o")
        ps_f = psum("ps_f")
        ps_a = psum("ps_a")
        ps_x = [psum("ps_x0"), psum("ps_x1")]
        ps_c = psum("ps_c")

        s_const = sem("s_const")
        s_prep = sem("s_prep")
        s_held = sem("s_held")
        s_bn = sem("s_bn")
        s_prepp = sem("s_prepp")
        s_xrow = sem("s_xrow")
        s_xtr = sem("s_xtr")
        s_xT = sem("s_xT")
        s_xp = sem("s_xp")
        s_patch = sem("s_patch")
        s_pst = sem("s_pst")
        s_patchfree = sem("s_patchfree")
        s_conv9 = sem("s_conv9")
        s_conv = sem("s_conv")
        s_hT = sem("s_hT")
        s_hTs = sem("s_hTs")
        s_co = sem("s_co")
        s_off = sem("s_off")
        s_offfree = sem("s_offfree")
        s_ix = sem("s_ix")
        s_ex = sem("s_ex")
        s_pub = sem("s_pub")
        s_gat = [sem("s_gat0"), sem("s_gat1")]
        s_xt = sem("s_xt")
        s_mlp = sem("s_mlp")
        s_mlp_pe = sem("s_mlp_pe")
        s_rstd = sem("s_rstd")
        s_rs2 = sem("s_rs2")
        s_gelu = sem("s_gelu")
        s_tst = sem("s_tst")
        s_tfree = sem("s_tfree")
        s_S = sem("s_S")
        s_E = sem("s_E")
        s_PV = sem("s_PV")
        s_tl = sem("s_tl")
        s_fin = sem("s_fin")
        s_z2T = sem("s_z2T")
        s_lg = sem("s_lg")
        s_lgc = sem("s_lgc")
        s_t2st = sem("s_t2st")
        s_t2free = sem("s_t2free")
        s_rt = sem("s_rt")
        s_rex = sem("s_rex")
        s_mpst = sem("s_mpst")
        s_zc = sem("s_zc")
        s_mpT = sem("s_mpT")
        s_mpTc = sem("s_mpTc")
        s_pool = sem("s_pool")
        s_w = [sem("s_w0"), sem("s_w1")]
        s_eh = sem("s_eh")
        s_ehg = sem("s_ehg")
        s_eo = sem("s_eo")
        s_eoc = sem("s_eoc")
        s_eT = sem("s_eT")
        s_eTc = sem("s_eTc")
        s_fl = [sem("s_fl0"), sem("s_fl1")]
        s_comb = sem("s_comb")
        s_res = sem("s_res")
        s_outst = [sem("s_outst0"), sem("s_outst1")]

        NCONST, PREP = 19, 9
        b1_row = w1.rearrange("(e d) h -> e d h", e=NE)[:, C, :]
        b2_row = w2.rearrange("(e d) h -> e d h", e=NE)[:, EF, :]
        w1_v = w1.rearrange("(e d) h -> e d h", e=NE)
        w2_v = w2.rearrange("(e d) h -> e d h", e=NE)
        spare = V1[:, 0].rearrange("p t c -> p (t c)")
        w1_s = spare[:, 0:2 * EF].rearrange("p (k h) -> p k h", k=2)
        w2_s = spare[:, 2 * EF:4 * EF].rearrange("p (k a c) -> p k a c", k=2, c=C)
        eoT = spare[:, 4 * EF:4 * EF + NI * NE].rearrange("p (n e) -> p n e", n=NI)
        eo = zT[0:NE, 0, 0:NI * C].rearrange("p (n c) -> p n c", n=NI)
        flat = [gat[:, i].rearrange("p a b c -> p (a b c)") for i in range(2)]
        t2c = [f[:, 0:RG * C].rearrange("p (a c) -> p a c", a=RG) for f in flat]
        res = [f[:, RG * C:2 * RG * C].rearrange("p (a c) -> p a c", a=RG) for f in flat]
        mpc = [f[0:NE, 2 * RG * C:3 * RG * C] for f in flat]

        def hold(eng):
            eng.sem_inc(s_held, 1)

        block = ctx.enter_context(nc.Block())

        @block.sync
        def _(sp):
            for dst, src in ((w_in_s[:], w_in), (b_in_s[:], b_in), (taps_s[:], taps), (chan_s[:], chan),
                             (w_om_s[:], w_om), (place_s[:], place), (b_om_s[:], b_om), (w_out_s[:], w_out),
                             (b_out_s[:], b_out), (aff_s[:], affine), (w_fc1_s[:], w_fc1), (b_fc1_s[:], b_fc1),
                             (w_fc2_s[:], w_fc2.rearrange("(a p) c -> p a c", p=128)), (b_fc2_s[:], b_fc2),
                             (gate_w_s[:], gate_wt), (gate_b_s[:], gate_b), (keep_s[:], keep),
                             (b1_s[:], b1_row), (b2_s[:], b2_row)):
                sp.dma_start(dst, src).then_inc(s_const, 16)
            sp.sem_inc(s_mpst, 16)
            sp.sem_inc(s_patchfree, 1)
            sp.sem_inc(s_tfree, 1)
            sp.sem_inc(s_t2free, 1)

            def step(s, A, B, D, rows, last):
                if rows:
                    r = s.rows(1)
                    sp.wait_ge(s_patch, r * 2 + 2)
                    hold(sp)
                    sp.dma_start(table_v[1 - s.par][:, :, bass.ds(s.t * (RS * 4 * CG), RS * 4 * CG)],
                                 patch[:].rearrange("x g k a b c -> x g (k a b c)")).then_inc(s_pst, 16)
                    sp.wait_ge(s_pst, (r + 1) * 16)
                    sp.sem_inc(s_patchfree, 1)
                if B:
                    i = s.tile()
                    sp.wait_ge(s_mlp, i * M_N + M_T)
                    hold(sp)
                    sp.dma_start(t_dram[bass.ds(i * TT, TT), :], tb[:]).then_inc(s_tst, 16)
                    sp.wait_ge(s_tst, (i + 1) * 16)
                    sp.sem_inc(s_tfree, 1)
                if D:
                    i = s.tile(-1)
                    sp.wait_ge(s_fin, i * F_N + F_Z2)
                    hold(sp)
                    sp.dma_start(t2_dram[bass.ds(i * TT, TT), :], t2[:]).then_inc(s_t2st, 16)
                    sp.dma_start(z2_dram[bass.ds(i * TT, TT), :], z2[:]).then_inc(s_t2st, 16)
                    sp.wait_ge(s_t2st, (i + 1) * 32)
                    sp.sem_inc(s_t2free, 1)

            def image_end(s):
                i = s.n - 1
                z2_v = z2_dram.rearrange("(n c a p) d -> n c p a d", n=NI, c=NC_OUT, p=TT)
                for c in range(NC_OUT):
                    if c:
                        sp.wait_ge(s_zc, i * (16 * NC_OUT) + 16 * c)
                        hold(sp)
                    if c >= 2:
                        sp.wait_ge(s_pool, i * NC_OUT + c - 1)
                        hold(sp)
                    sp.dma_start(zc[:, c % 2], z2_v[bass.ds(i, 1), c].rearrange("o p a d -> (o p) a d"))\
                        .then_inc(s_zc, 16)
                sp.wait_ge(s_rt, i * R_N + R_MP)
                hold(sp)
                sp.dma_start(mp_dram[bass.ds(i * NE, NE), :], picked[:]).then_inc(s_mpst, 16)

            walk(sp, step, image_end)

            with sp.Fori(0, NE // 2) as u:
                for k in range(2):
                    e = u * 2 + k
                    sp.wait_ge(s_eoc, e + 1)
                    hold(sp)
                    sp.dma_start(w1_s[:, k, :], w1_v[bass.ds(e, 1), 0:C, :].rearrange("o p h -> (o p) h"))\
                        .then_inc(s_w[k], 16)
                    sp.dma_start(w2_s[:, k], w2_v[bass.ds(e, 1), 0:EF, :]
                                 .rearrange("o (a p) c -> p (o a) c", p=128)).then_inc(s_w[k], 16)

            t2_v = t2_dram.rearrange("(q a p) d -> q p a d", a=RG, p=TT)
            out_v = out.rearrange("(n l) d -> n l d", n=NI)
            mp_v = mp_dram.rearrange("(n e) (c l) -> n e c l", n=NI, c=NC_OUT)
            sp.wait_ge(s_mpst, 16 * NI + 16)

            def load(m, q):
                if q >= 2 * NC_OUT:
                    m, q = m + 1, q - 2 * NC_OUT
                n = m * 2 + q // NC_OUT
                sp.dma_start(t2c[q % 2], t2_v[bass.ds(m * (2 * NC_OUT) + q, 1)].rearrange("o p a d -> (o p) a d"))\
                    .then_inc(s_fl[q % 2], 16)
                sp.dma_start(mpc[q % 2], mp_v[bass.ds(n, 1), :, q % NC_OUT, :].rearrange("o e l -> (o e) l"))\
                    .then_inc(s_fl[q % 2], 16)

            def store(m, q):
                n, c = m * 2 + q // NC_OUT, q % NC_OUT
                full = RG if c < NC_OUT - 1 else RG - 1
                sp.wait_ge(s_res, m * (2 * NC_OUT) + q + 1)
                hold(sp)
                sp.dma_start(out_v[bass.ds(n, 1), c * RG * TT:(c * RG + full) * TT, :]
                             .rearrange("o (a p) d -> p (o a) d", p=TT), res[q % 2][:, 0:full, :])\
                    .then_inc(s_outst[q % 2], 16)
                if full < RG:
                    sp.dma_start(out_v[bass.ds(n, 1), (NT - 1) * TT:L, :].rearrange("o p d -> (o p) d"),
                                 res[q % 2][0:TAIL, RG - 1, :]).then_inc(s_outst[q % 2], 16)

            load(0, 0)
            load(0, 1)
            def pair(m, end):
                for q in range(2 * NC_OUT):
                    store(m, q)
                    if not end or q + 2 < 2 * NC_OUT:
                        load(m, q + 2)
            with sp.Fori(0, NI // 2 - 1) as m:
                pair(m, False)
            pair(NI // 2 - 1, True)
            sp.wait_ge(s_outst[0], 16 * 6 * (NI // 2))
            sp.wait_ge(s_outst[1], 16 * 6 * (NI // 2))

        @block.gpsimd
        def _(pool):
            pool.memset(ident[:], 0.0).then_inc(s_prepp, 1)
            pool.wait_ge(s_prepp, 1)
            pool.affine_select(out=ident[:], in_=ident[:], compare_op=ALU.not_equal, fill=1.0, base=0,
                               pattern=[[-1, 128]], channel_multiplier=1).then_inc(s_prepp, 1)

            def tile(s):
                k = s.slot
                pool.wait_ge(s_pub, s.tile() + 1)
                hold(pool)
                for j in range(GP):
                    pool.indirect_dma_start(gat[:, k, j].rearrange("p a c -> p (a c)"), None, table[s.par],
                                            bass.IndirectOffsetOnAxis(ap=idx_now[:, k, j:j + 1], axis=0))\
                        .then_inc(s_gat[k], 16)

            with pool.Fori(0, NI // 2) as m:
                for par in range(2):
                    with pool.Fori(0, NT // 2) as u:
                        for k in range(2):
                            tile(Step(m, par, u, k))
                    tile(Step(m, par, NT // 2, 0))

        @block.tensor
        def _(pe):
            pe.wait_ge(s_const, 16 * NCONST)
            pe.wait_ge(s_prepp, 2)
            pe.wait_ge(s_prep, PREP)

            def row_step(s):
                r, i, k = s.rows(1), s.tile(1), s.k
                pe.wait_ge(s_xrow, r * 32 + 32)
                pe.wait_ge(s_offfree, i + 1)
                for j in range(3):
                    last = pe.transpose(ps_a[:, j * XR:(j + 1) * XR], xrow[:, k, j, :], ident[0:XR, 0:XR])
                last.then_inc(s_xtr, 1)
                pe.wait_ge(s_xT, r + 1)
                for h in range(2):
                    for j in range(2):
                        for dx in range(2):
                            row = 2 * h + j
                            o = ps_x[h][0:PX, (2 * j + dx) * C:(2 * j + dx + 1) * C]
                            pe.matmul(o, xT[:, row, dx:dx + PX], w_in_s[:], start=True, stop=False)
                            last = pe.matmul(o, prow[0:1, k, row * WP + dx:row * WP + dx + PX], b_in_s[:],
                                             start=False, stop=True)
                    last.then_inc(s_xp, 1)

            def offsets(s, rows):
                i = s.tile(1)
                pe.wait_ge(s_hTs, i + 1)
                pe.wait_ge(s_co, i * 16 + 16)
                if not rows:
                    pe.wait_ge(s_offfree, i + 1)
                o = ps_a[:, 3 * XR:3 * XR + 4 * GP]
                pe.matmul(o, hTs[:], w_om_s[:], start=True, stop=False)
                pe.matmul(o, co[:, s.slot ^ 1, :], place_s[:], start=False, stop=True).then_inc(s_off, 1)

            def attention(s):
                b, i = 1 - s.par, s.tile(-1)
                pe.wait_ge(s_mlp, s.m * (2 * NT * M_N) + s.par * NT * M_N)
                def pv(g):
                    pe.wait_ge(s_E, i * NG + g + 1)
                    for j in range(g * KT, min(g * KT + KT, NT)):
                        last = pe.matmul(ps_o[:, 0:C + 1], E[:, g % 2, (j % KT) * TT:(j % KT + 1) * TT],
                                         V1[:, b, j, :], start=(j == 0), stop=(j == NT - 1))
                    last.then_inc(s_PV, 1)
                for g in range(NG):
                    if g >= 2:
                        pe.wait_ge(s_E, i * NG + g - 1)
                    for j in range(g * KT, min(g * KT + KT, NT)):
                        last = pe.matmul(ps_s[g % 2][:, (j % KT) * TT:(j % KT + 1) * TT],
                                         zT[:, b, j * TT:(j + 1) * TT], zT[:, b, bass.ds(s.t * TT, TT)],
                                         start=True, stop=True)
                    last.then_inc(s_S, 1)
                    if g:
                        pv(g - 1)
                pv(NG - 1)

            def block_tail(s):
                i = s.tile()
                d, q = i * M_N, ps_c
                pe.wait_ge(s_mlp, d + M_Y)
                pe.transpose(q[:, 0:TT], y[:], ident[:]).then_inc(s_mlp_pe, 1)
                pe.wait_ge(s_mlp, d + M_YT)
                pe.matmul(q[:, TT:TT + C], yT[:], w_out_s[:], start=True, stop=False)
                pe.matmul(q[:, TT:TT + C], ones[:], b_out_s[:], start=False, stop=True).then_inc(s_mlp_pe, 1)
                pe.wait_ge(s_mlp, d + M_X1)
                pe.transpose(q[:, 2 * TT:3 * TT], x1[:], ident[:]).then_inc(s_mlp_pe, 1)
                pe.wait_ge(s_mlp, d + M_X1T)
                for f in range(FF // 128):
                    o = q[:, f * TT:(f + 1) * TT]
                    pe.matmul(o, w_fc1_s[:, f * 128:(f + 1) * 128], x1T[:], start=True, stop=False)
                    last = pe.matmul(o, b_fc1_s[:, f * 128:(f + 1) * 128], ones[:], start=False, stop=True)
                last.then_inc(s_mlp_pe, 1)
                pe.wait_ge(s_gelu, i + 1)
                for f in range(FF // 128):
                    pe.matmul(q[:, 0:C], hs[:, f * TT:(f + 1) * TT], w_fc2_s[:, f, :], start=(f == 0), stop=False)
                pe.matmul(q[:, 0:C], ones[:], b_fc2_s[:], start=False, stop=True).then_inc(s_mlp_pe, 1)
                pe.wait_ge(s_mlp, d + M_ZN)
                pe.transpose(q[:, TT:2 * TT], zn[:], ident[:]).then_inc(s_mlp_pe, 1)

            def router_logits(s):
                i = s.tile(-1)
                pe.wait_ge(s_fin, i * F_N + F_Z2)
                pe.transpose(ps_f[:, 0:TT], z2[:], ident[:]).then_inc(s_z2T, 1)
                pe.wait_ge(s_fin, i * F_N + F_Z2T)
                o = ps_f[0:NE, TT:2 * TT]
                pe.matmul(o, gate_w_s[:], z2T[:], start=True, stop=False)
                pe.matmul(o, gate_b_s[:], ones[:], start=False, stop=True).then_inc(s_lg, 1)

            def step(s, A, B, D, rows, last):
                if rows:
                    row_step(s)
                if D:
                    attention(s)
                if B:
                    block_tail(s)
                if D:
                    router_logits(s)
                if A:
                    offsets(s, rows)

            def image_end(s):
                n = s.n - 1
                pe.wait_ge(s_lgc, n * NT + NT)
                pe.wait_ge(s_rt, n * R_N + R_MP)
                hold(pe)
                for c in range(NC_OUT):
                    for a in range(RG):
                        j = c * RG + a
                        last = pe.transpose(ps_f[:, a * NE:(a + 1) * NE], picked[:, j * TT:(j + 1) * TT],
                                            ident[0:NE, 0:NE])
                    last.then_inc(s_mpT, 1)
                    pe.wait_ge(s_mpTc, n * NC_OUT + c + 1)
                    pe.wait_ge(s_zc, n * (16 * NC_OUT) + 16 * (c + 1))
                    for a in range(RG):
                        last = pe.matmul(ps_o[:, 0:NE], zc[:, c % 2, a, :], mpT[:, a, :],
                                         start=(c == 0 and a == 0), stop=(c == NC_OUT - 1 and a == RG - 1))
                    last.then_inc(s_pool, 1)
                pe.wait_ge(s_rt, n * R_N + R_N)
                hold(pe)

            walk(pe, step, image_end)

            pe.wait_ge(s_rt, NI * R_N)
            with pe.Fori(0, NE // 2) as u:
                for k in range(2):
                    e = u * 2 + k
                    pe.wait_ge(s_w[k], u * 32 + 32)
                    pe.wait_ge(s_ehg, e + 1)
                    hold(pe)
                    for f in range(EF // 128):
                        o = ps_s[0][:, f * NI:(f + 1) * NI]
                        pe.matmul(o, w1_s[:, k, f * 128:(f + 1) * 128], pooled[:, :, bass.ds(e, 1)],
                                  start=True, stop=False)
                        last = pe.matmul(o, b1_s[:, f * 128:(f + 1) * 128],
                                         ident[0:NE, bass.ds(e, 1)].to_broadcast([NE, NI]), start=False, stop=True)
                    last.then_inc(s_eh, 1)
                    pe.wait_ge(s_ehg, e + 2)
                    pe.wait_ge(s_eoc, e + 2)
                    hold(pe)
                    o = ps_o[:, 0:NI]
                    for f in range(EF // 128):
                        pe.matmul(o, w2_s[:, k, f, :], eh[:, f, :], start=(f == 0), stop=False)
                    pe.matmul(o, b2_s[:], ident[0:NE, bass.ds(e, 1)].to_broadcast([NE, NI]),
                              start=False, stop=True).then_inc(s_eo, 1)
            pe.wait_ge(s_eoc, NE + 2)
            for n in range(NI):
                b = ps_x[n // 4]
                last = pe.transpose(b[0:NE, (n % 4) * C:(n % 4 + 1) * C], eoT[:, n, :], ident[:])
            last.then_inc(s_eT, 1)
            pe.wait_ge(s_eTc, 1)
            with pe.Fori(0, NI // 2) as m:
                for q in range(2 * NC_OUT):
                    v = m * (2 * NC_OUT) + q
                    pe.wait_ge(s_fl[q % 2], m * (32 * NC_OUT) + 32 * (q // 2 + 1))
                    if q:
                        pe.wait_ge(s_res, v)
                    hold(pe)
                    for a in range(RG):
                        o = (ps_s if q % 2 else ps_x)[a // 4][:, (a % 4) * C:(a % 4 + 1) * C]
                        last = pe.matmul(o, mpc[q % 2][:, a * TT:(a + 1) * TT],
                                         eo[:, bass.ds(m * 2 + q // NC_OUT, 1), :].rearrange("e o c -> e (o c)"),
                                         start=True, stop=True)
                    last.then_inc(s_comb, 1)

        @block.scalar
        def _(act):
            def load_rows(r, k):
                act.dma_start(xrow[:, k], xpad[bass.ds(r * (RS * WP), 3 * XR), :]
                              .rearrange("(k p) c -> p k c", p=XR)).then_inc(s_xrow, 16)
                act.dma_start(prow[0:1, k, :], padmask[0:1, bass.ds(r * (RS * WP), 4 * WP)]).then_inc(s_xrow, 16)

            def load_coords(i, k):
                act.dma_start(co[:, k, :], coords[:, bass.ds(i * TT, TT)]).then_inc(s_co, 16)

            load_rows(0, 0)
            load_coords(0, 0)
            def root(mean_var, r, tmp, s_own, at):
                act.activation(tmp, mean_var[:, 1:2], ACT.Ln, bias=eps[:, 0:1]).then_inc(s_own, 1)
                act.wait_ge(s_own, at + 1)
                act.activation(r, tmp, ACT.Exp, scale=-0.5).then_inc(s_own, 1)

            act.wait_ge(s_const, 16 * NCONST)
            act.wait_ge(s_prep, 4)
            root(chan_s[:, 3:5], bn[:, 3:4], bn[:, 2:3], s_bn, 0)
            act.wait_ge(s_prep, PREP)

            def step(s, A, B, D, rows, last):
                r, ia = s.rows(1), s.tile(1)
                if rows:
                    act.wait_ge(s_xrow, r * 32 + 32)
                    load_rows(r + 1, 1 - s.k)
                if A:
                    act.wait_ge(s_co, ia * 16 + 16)
                    load_coords(ia + 1, s.slot)
                if B:
                    act.dma_start(xt[:], xtok[bass.ds(s.tile() * TT, TT), :]).then_inc(s_xt, 16)
                if D:
                    act.wait_ge(s_tfree, s.m * (2 * NT) + NT * s.par + 1)
                    act.dma_start(tl[:], t_dram[bass.ds(s.tile(-1) * TT, TT), :]).then_inc(s_tl, 16)
                if rows:
                    act.wait_ge(s_xtr, r + 1)
                    act.copy(xT[:].rearrange("p a b -> p (a b)"), ps_a[:, 0:3 * XR]).then_inc(s_xT, 1)
                    act.wait_ge(s_patchfree, r + 1)
                    for row in range(4):
                        if row % 2 == 0:
                            act.wait_ge(s_xp, r * 2 + row // 2 + 1)
                        src = ps_x[row // 2][0:PX, (row % 2) * 2 * C:(row % 2 + 1) * 2 * C]\
                            .rearrange("p (d g c) -> p d g c", d=2, g=GR)
                        for kk, dy in ((row, 0), (row - 1, 1)):
                            if 0 <= kk < RS:
                                end = act.copy(patch[:, :, kk, :, dy, :].rearrange("p g d c -> p d g c"), src)
                        if row % 2:
                            end.then_inc(s_patch, 1)
                if D:
                    i = s.tile(-1)
                    for g in range(NG):
                        w = min(KT, NT - g * KT) * TT
                        act.wait_ge(s_S, i * NG + g + 1)
                        if g >= 2:
                            act.wait_ge(s_PV, i * NG + g - 1)
                        act.activation(E[:, g % 2, 0:w], ps_s[g % 2][:, 0:w], ACT.Exp, bias=nshift[:, 0:1])\
                            .then_inc(s_E, 1)
                if B:
                    i = s.tile()
                    act.wait_ge(s_mlp, i * M_N + M_AG1)
                    root(mv, rstd[:], lnv[:, 0:1], s_rstd, i * 6)
                    act.wait_ge(s_mlp_pe, i * P_N + P_FC1)
                    act.activation(hs[:], ps_c[:], ACT.Gelu).then_inc(s_gelu, 1)
                if rows:
                    act.wait_ge(s_conv, r + 1)
                    act.activation(hT[:, bass.ds(s.t * (RS * WW), RS * WW)], acc[:].rearrange("p a b -> p (a b)"),
                                   ACT.Gelu, bias=bn[:, 1:2], scale=bn[:, 0:1]).then_inc(s_hT, 1)
                if B:
                    i = s.tile()
                    act.wait_ge(s_mlp, i * M_N + M_AG2)
                    root(mv, rstd[:], lnv[:, 0:1], s_rstd, i * 6 + 2)
                    act.wait_ge(s_mlp, i * M_N + M_AG3)
                    root(mv, rstd[:], lnv[:, 0:1], s_rstd, i * 6 + 4)
                if D:
                    i = s.tile(-1)
                    act.wait_ge(s_fin, i * F_N + F_AG)
                    root(mv2, rs2[:], lnv[:, 1:2], s_rs2, i * 2)
                    act.wait_ge(s_lg, i + 1)
                    act.copy(probs[:, bass.ds(s.t * TT, TT)], ps_f[0:NE, TT:2 * TT]).then_inc(s_lgc, 1)
                if A:
                    if rows:
                        act.wait_ge(s_hT, r + 1)
                    act.copy(hTs[:], hT[:, bass.ds(s.t * TT, TT)]).then_inc(s_hTs, 1)
                    act.wait_ge(s_ix, ia * I_N + I_SUB)
                    act.activation(ex[:], ex[:], ACT.Exp).then_inc(s_ex, 1)

            def image_end(s):
                n = s.n - 1
                act.wait_ge(s_rt, n * R_N + R_NM)
                act.activation(probs[:, 0:L], probs[:, 0:L], ACT.Exp, bias=rt[:, 1:2], accum_out=rt[:, 2:3])\
                    .then_inc(s_rex, 1)
                for c in range(NC_OUT):
                    act.wait_ge(s_mpT, n * NC_OUT + c + 1)
                    act.copy(mpT[:].rearrange("p a e -> p (a e)"), ps_f[:, 0:RG * NE]).then_inc(s_mpTc, 1)

            walk(act, step, image_end)

            act.sem_inc(s_ehg, 1)
            with act.Fori(0, NE) as e:
                act.wait_ge(s_eh, e + 1)
                act.activation(eh[:].rearrange("p a n -> p (a n)"), ps_s[0][:, 0:EF // 128 * NI], ACT.Gelu)\
                    .then_inc(s_ehg, 1)
            act.wait_ge(s_xrow, 32 * (NI * NR + 1))
            act.wait_ge(s_co, 16 * (NI * NT + 1))

        @block.vector
        def _(v):
            v.memset(ones[:], 1.0).then_inc(s_prep, 1)
            v.memset(nshift[:], -SHIFT).then_inc(s_prep, 1)
            v.memset(picked[:, L:LP], 0.0).then_inc(s_prep, 1)
            v.wait_ge(s_const, 16 * NCONST)
            v.memset(eps[:], EPS).then_inc(s_prep, 1)
            v.wait_ge(s_bn, 2)
            v.tensor_tensor(bn[:, 0:1], bn[:, 3:4], chan_s[:, 1:2], ALU.mult)
            v.tensor_tensor(bn[:, 2:3], chan_s[:, 0:1], chan_s[:, 3:4], ALU.subtract).then_inc(s_prep, 1)
            v.wait_ge(s_prep, 5)
            v.scalar_tensor_tensor(out=bn[:, 1:2], in0=bn[:, 2:3], scalar=bn[:, 0:1], in1=chan_s[:, 2:3],
                                   op0=ALU.mult, op1=ALU.add).then_inc(s_prep, 1)
            v.tensor_tensor(place_s[0:1, :], place_s[0:1, :], b_om_s[:], ALU.add).then_inc(s_prep, 1)
            for b in range(2):
                last = v.tensor_copy(V1[:, b, :, C:C + 1], keep_s[:].unsqueeze(2))
            last.then_inc(s_prep, 1)
            for gamma, rows in ((0, (1, 2)), (3, (4, 5))):
                for i in rows:
                    last = v.tensor_tensor(aff_s[:, i, :], aff_s[:, i, :], aff_s[:, gamma, :], ALU.mult)
            last.then_inc(s_prep, 1)
            v.wait_ge(s_prep, PREP)
            v.sem_inc(s_offfree, 1)
            v.sem_inc(s_eoc, 2)

            def publish(n, t, slot):
                v.tensor_copy(idx_now[:, slot, :], idx[:, bass.ds(t, 1), :].rearrange("p o j -> p (o j)"))\
                    .then_inc(s_pub, 1)

            def conv(s):
                r = s.rows(1)
                v.wait_ge(s_xT, r + 1)
                for tap in range(PT):
                    src = xT[:, tap // 3:tap // 3 + RS, tap % 3:tap % 3 + WW]
                    if tap == 0:
                        v.tensor_scalar(acc[:], src, taps_s[:, 0:1], None, ALU.mult).then_inc(s_conv9, 1)
                    else:
                        v.wait_ge(s_conv9, r * 8 + tap)
                        last = v.scalar_tensor_tensor(out=acc[:], in0=src, scalar=taps_s[:, tap:tap + 1],
                                                      in1=acc[:], op0=ALU.mult, op1=ALU.add)
                        last.then_inc(s_conv9 if tap < 8 else s_conv, 1)

            def stats_of(src, stats, mean_var, s_own, at):
                v.bn_stats(stats[:], src).then_inc(s_own, 1)
                v.wait_ge(s_own, at + 1)
                hold(v)
                v.bn_aggr(mean_var[:], stats[:]).then_inc(s_own, 1)
                v.wait_ge(s_own, at + 2)

            def block_tail(s):
                i, slot = s.tile(), s.slot
                d, p = i * M_N, i * P_N
                v.wait_ge(s_xt, i * 16 + 16)
                v.tensor_tensor(xb[:], xt[:], B1, ALU.add).then_inc(s_mlp, 1)
                v.wait_ge(s_gat[slot], (s.half() + 1) * (16 * GP))
                g = gat[:, slot].rearrange("p j k c -> p (j k) c")
                w = wts[:, bass.ds(s.t, 1)].rearrange("p o j a b -> p (o j a b)")
                v.tensor_tensor(g, g, w.unsqueeze(2).to_broadcast([128, 4 * GP, CG]), ALU.mult).then_inc(s_mlp, 1)
                v.wait_ge(s_mlp, d + M_MUL)
                v.tensor_reduce(y[:].rearrange("p (g c) -> p g c", g=GR),
                                gat[:, slot].rearrange("p (g j) k c -> p g c (j k)", g=GR), AX.X, ALU.add)\
                    .then_inc(s_mlp, 1)
                v.wait_ge(s_mlp_pe, p + P_YT)
                v.tensor_copy(yT[:], ps_c[:, 0:TT]).then_inc(s_mlp, 1)
                v.wait_ge(s_mlp_pe, p + P_OUT)
                stats_of(ps_c[:, TT:TT + C], st, mv, s_mlp, d + M_YT)
                v.wait_ge(s_rstd, i * 6 + 2)
                v.tensor_scalar(z[:], ps_c[:, TT:TT + C], mv[:, 0:1], rstd[:, 0:1], ALU.subtract, ALU.mult)\
                    .then_inc(s_mlp, 1)
                v.wait_ge(s_mlp, d + M_Z1)
                v.tensor_tensor(za[:], z[:], A1, ALU.mult).then_inc(s_mlp, 1)
                v.wait_ge(s_mlp, d + M_ZA1)
                v.tensor_tensor(x1[:], za[:], xb[:], ALU.add).then_inc(s_mlp, 1)
                v.wait_ge(s_mlp_pe, p + P_X1T)
                v.tensor_copy(x1T[:], ps_c[:, 2 * TT:3 * TT]).then_inc(s_mlp, 1)
                v.tensor_tensor(x1b[:], x1[:], B2, ALU.add).then_inc(s_mlp, 1)
                v.wait_ge(s_mlp_pe, p + P_FC2)
                stats_of(ps_c[:, 0:C], st, mv, s_mlp, d + M_X1B)
                v.wait_ge(s_rstd, i * 6 + 4)
                v.tensor_scalar(z[:], ps_c[:, 0:C], mv[:, 0:1], rstd[:, 0:1], ALU.subtract, ALU.mult)\
                    .then_inc(s_mlp, 1)
                v.wait_ge(s_mlp, d + M_Z2)
                v.tensor_tensor(za[:], z[:], A2, ALU.mult).then_inc(s_mlp, 1)
                v.wait_ge(s_mlp, d + M_ZA2)
                v.wait_ge(s_tfree, i + 1)
                v.tensor_tensor(tb[:], za[:], x1b[:], ALU.add).then_inc(s_mlp, 1)
                v.wait_ge(s_mlp, d + M_T)
                stats_of(tb[:], st, mv, s_mlp, d + M_T)
                v.wait_ge(s_rstd, i * 6 + 6)
                v.tensor_tensor(rstm[:], rstd[:], keep_s[:, bass.ds(s.t, 1)], ALU.mult).then_inc(s_mlp, 1)
                v.wait_ge(s_mlp, d + M_RSM)
                v.tensor_scalar(zn[:], tb[:], mv[:, 0:1], rstm[:, 0:1], ALU.subtract, ALU.mult).then_inc(s_mlp, 1)
                v.wait_ge(s_mlp, d + M_ZN)
                v.tensor_copy(V1[:, s.par, bass.ds(s.t, 1), 0:C], zn[:].unsqueeze(1)).then_inc(s_mlp, 1)
                v.wait_ge(s_mlp_pe, p + P_ZT)
                v.tensor_copy(zT[:, s.par, bass.ds(s.t * TT, TT)], ps_c[:, TT:2 * TT]).then_inc(s_mlp, 1)

            def attention_end(s):
                i = s.tile(-1)
                d = i * F_N
                v.wait_ge(s_PV, i * NG + NG)
                v.reciprocal(rc[:], ps_o[:, C:C + 1]).then_inc(s_fin, 1)
                v.wait_ge(s_tl, i * 16 + 16)
                v.wait_ge(s_t2free, i + 1)
                v.wait_ge(s_fin, d + F_RC)
                v.scalar_tensor_tensor(out=t2[:], in0=ps_o[:, 0:C], scalar=rc[:, 0:1], in1=tl[:],
                                       op0=ALU.mult, op1=ALU.add).then_inc(s_fin, 1)
                v.wait_ge(s_fin, d + F_T2)
                stats_of(t2[:], st2, mv2, s_fin, d + F_T2)
                v.wait_ge(s_rs2, i * 2 + 2)
                v.tensor_scalar(z2[:], t2[:], mv2[:, 0:1], rs2[:, 0:1], ALU.subtract, ALU.mult).then_inc(s_fin, 1)
                v.wait_ge(s_z2T, i + 1)
                v.tensor_copy(z2T[:], ps_f[:, 0:TT]).then_inc(s_fin, 1)

            def indices(s):
                i = s.tile(1)
                d = i * I_N
                o = ps_a[:, 3 * XR:3 * XR + 4 * GP]
                v.wait_ge(s_off, i + 1)
                v.tensor_scalar(cc[:], o[:, 0:2 * GP], 0.0, TMAX, ALU.max, ALU.min).then_inc(s_ix, 1)
                lg = o[:, 2 * GP:3 * GP].rearrange("p (g j) -> p g j", g=GR)
                e3 = ex[:].rearrange("p (g j) -> p g j", g=GR)
                v.tensor_reduce(sm[:, 0, :], lg, AX.X, ALU.max).then_inc(s_ix, 1)
                v.wait_ge(s_ix, d + I_MX)
                v.tensor_tensor(e3, lg, sm[:, 0, :].unsqueeze(2).to_broadcast([128, GR, PT]), ALU.subtract)\
                    .then_inc(s_ix, 1)
                v.tensor_copy(ri[:], cc[:]).then_inc(s_ix, 1)
                v.wait_ge(s_ix, d + I_RI)
                v.tensor_copy(rf[:], ri[:]).then_inc(s_ix, 1)
                v.wait_ge(s_ix, d + I_RF)
                v.tensor_tensor(gt[:], rf[:], cc[:], ALU.is_gt).then_inc(s_ix, 1)
                v.wait_ge(s_ix, d + I_GT)
                v.tensor_tensor(fl[:], rf[:], gt[:], ALU.subtract).then_inc(s_ix, 1)
                v.wait_ge(s_ix, d + I_FL)
                v.tensor_scalar(fl[:], fl[:], TMAX - 1.0, None, ALU.min).then_inc(s_ix, 1)
                v.wait_ge(s_ix, d + I_FM)
                v.tensor_tensor(frac[:, :, 1], cc[:], fl[:], ALU.subtract).then_inc(s_ix, 1)
                v.wait_ge(s_ix, d + I_FR)
                v.tensor_scalar(frac[:, :, 0], frac[:, :, 1], -1.0, 1.0, ALU.mult, ALU.add).then_inc(s_ix, 1)
                v.scalar_tensor_tensor(out=ti[:], in0=fl[:, 0:GP], scalar=float(PY), in1=fl[:, GP:2 * GP],
                                       op0=ALU.mult, op1=ALU.add).then_inc(s_ix, 1)
                v.wait_ge(s_ix, d + I_TI)
                v.scalar_tensor_tensor(out=idx[:, bass.ds(s.t, 1), :].rearrange("p o j -> p (o j)"), in0=ti[:],
                                       scalar=0.25, in1=o[:, 3 * GP:4 * GP], op0=ALU.add, op1=ALU.add)\
                    .then_inc(s_ix, 1)
                v.wait_ge(s_ix, d + I_IDX)
                v.sem_inc(s_offfree, 1)
                v.wait_ge(s_ex, i + 1)
                v.tensor_reduce(sm[:, 1, :], e3, AX.X, ALU.add).then_inc(s_ix, 1)
                v.wait_ge(s_ix, d + I_SM)
                v.reciprocal(sm[:, 2, :], sm[:, 1, :]).then_inc(s_ix, 1)
                v.wait_ge(s_ix, d + I_RC)
                v.tensor_tensor(mk[:].rearrange("p (g j) -> p g j", g=GR), e3,
                                sm[:, 2, :].unsqueeze(2).to_broadcast([128, GR, PT]), ALU.mult).then_inc(s_ix, 1)
                v.wait_ge(s_ix, d + I_MK)
                v.tensor_tensor(wy[:], mk[:].unsqueeze(2).to_broadcast([128, GP, 2]), frac[:, GP:2 * GP, :],
                                ALU.mult).then_inc(s_ix, 1)
                v.wait_ge(s_ix, d + I_WY)
                v.tensor_tensor(wts[:, bass.ds(s.t, 1)].rearrange("p o j a b -> p (o j) a b"),
                                frac[:, 0:GP, :].unsqueeze(3).to_broadcast([128, GP, 2, 2]),
                                wy[:].unsqueeze(2).to_broadcast([128, GP, 2, 2]), ALU.mult).then_inc(s_ix, 1)

            def step(s, A, B, D, rows, last):
                if B:
                    if not last:
                        publish(s.n, s.t + 1, 1 - s.slot)
                    elif A:
                        v.wait_ge(s_patchfree, s.m * (2 * NR) + NR * (s.par + 2) + 1)
                        publish(s.n + 1, 0, 1 - s.slot)
                if rows:
                    conv(s)
                if B:
                    block_tail(s)
                if D:
                    attention_end(s)
                if A:
                    indices(s)
                if last and not B and A:
                    v.wait_ge(s_patchfree, NR + 1)
                    v.wait_ge(s_ix, NT * I_N)
                    publish(0, 0, 0)

            def image_end(s):
                n = s.n - 1
                d = n * R_N
                p, k = probs[:, 0:L], picked[:, 0:L]
                v.wait_ge(s_lgc, n * NT + NT)
                v.tensor_reduce(rt[:, 0:1], p, AX.X, ALU.max).then_inc(s_rt, 1)
                v.wait_ge(s_rt, d + R_MX)
                v.tensor_scalar(rt[:, 1:2], rt[:, 0:1], -1.0, None, ALU.mult).then_inc(s_rt, 1)
                v.wait_ge(s_rex, n + 1)
                v.reciprocal(rt[:, 3:4], rt[:, 2:3]).then_inc(s_rt, 1)
                v.wait_ge(s_rt, d + R_RC)
                v.tensor_scalar(p, p, rt[:, 3:4], None, ALU.mult).then_inc(s_rt, 1)
                v.wait_ge(s_rt, d + R_P)
                hold(v)
                v.max(top8[:], p).then_inc(s_rt, 1)
                v.wait_ge(s_rt, d + R_M8)
                v.wait_ge(s_mpst, n * 16 + 16)
                hold(v)
                v.match_replace(k, top8[:], p, -1.0).then_inc(s_rt, 1)
                v.wait_ge(s_rt, d + R_MR)
                v.scalar_tensor_tensor(out=k, in0=k, scalar=0.0, in1=p, op0=ALU.is_lt, op1=ALU.mult)\
                    .then_inc(s_rt, 1)
                v.wait_ge(s_pool, n * NC_OUT + NC_OUT)
                v.tensor_copy(pooled[:, bass.ds(n, 1), :], ps_o[:, 0:NE].unsqueeze(1)).then_inc(s_rt, 1)

            walk(v, step, image_end)

            with v.Fori(0, NE) as e:
                v.wait_ge(s_eo, e + 1)
                v.tensor_copy(eoT[:, :, bass.ds(e, 1)], ps_o[:, 0:NI].unsqueeze(2)).then_inc(s_eoc, 1)
            v.wait_ge(s_eT, 1)
            for h in range(2):
                last = v.tensor_copy(eo[:, 4 * h:4 * h + 4, :].rearrange("e n c -> e (n c)"), ps_x[h][0:NE, :])
            last.then_inc(s_eTc, 1)
            with v.Fori(0, NI // 2) as m:
                for q in range(2 * NC_OUT):
                    w = m * (2 * NC_OUT) + q
                    v.wait_ge(s_comb, w + 1)
                    if q >= 2:
                        done = sum(2 if x % NC_OUT == NC_OUT - 1 else 1 for x in range(q) if x % 2 == q % 2)
                        v.wait_ge(s_outst[q % 2], m * 96 + 16 * done)
                    b = ps_s if q % 2 else ps_x
                    v.tensor_tensor(res[q % 2][:, 0:4, :].rearrange("p a c -> p (a c)"), b[0][:],
                                    t2c[q % 2][:, 0:4, :].rearrange("p a c -> p (a c)"), ALU.add)
                    v.tensor_tensor(res[q % 2][:, 4, :], b[1][:, 0:C], t2c[q % 2][:, 4, :], ALU.add)\
                        .then_inc(s_res, 1)


def _constants():
    tok = np.arange(LP)
    real = tok < L
    one = np.stack([np.ones(LP), np.where(real, tok % WW + 1, 1), np.where(real, tok // WW + 1, 1)])
    coords = np.concatenate([np.tile(one, (1, NI)), one[:, :TT]], 1).astype(np.float32)
    place = np.zeros((3, 4 * GP), np.float32)
    point = np.tile(np.arange(PT), GR)
    place[0, 0:GP], place[0, GP:2 * GP] = point // 3 - 1, point % 3 - 1
    place[1, 0:GP] = 1
    place[2, GP:2 * GP] = 1
    place[0, 3 * GP:] = np.repeat(np.arange(GR), PT) * (PX * PY)
    mask = np.zeros((NI, HP, WP), np.float32)
    mask[:, 1:HH + 1, 1:WW + 1] = 1
    mask = np.concatenate([mask.reshape(-1), np.zeros(2 * RS * WP, np.float32)])
    keep = (np.arange(TT)[:, None] + np.arange(NT)[None] * TT < L).astype(np.float32)
    return coords, place, mask.reshape(1, -1), keep


def kernel(**inputs):
    import concourse.bacc as _bacc
    from concourse.bass_utils import run_bass_kernel_spmd as _run

    a = {k.removeprefix("L0_conv_"): np.asarray(v) for k, v in inputs.items()}
    x = a["x"]
    coords, place, mask, keep = _constants()
    row = lambda v: v.reshape(1, -1)
    xpad = np.zeros((NI, HP, WP, C), x.dtype)
    xpad[:, 1:HH + 1, 1:WW + 1] = x
    xtok = np.zeros((NI, LP, C), x.dtype)
    xtok[:, :L] = x.reshape(NI, L, C)
    w_off, b_off = a["w_off"].reshape(C, GP, 2), a["b_off"].reshape(GP, 2)
    zero = np.zeros((C, GP), x.dtype)
    arrays = {
        "xpad": np.concatenate([xpad.reshape(-1, C), np.zeros((2 * RS * WP, C), x.dtype)]),
        "xtok": xtok.reshape(-1, C),
        "padmask": mask,
        "coords": coords,
        "w_in": a["w_in"], "b_in": row(a["b_in"]),
        "taps": a["dw_w"].reshape(C, PT),
        "chan": np.stack([a["dw_b"], a["bn_g"], a["bn_b"], a["bn_m"], a["bn_v"]], 1),
        "w_om": np.concatenate([w_off[..., 0], w_off[..., 1], a["w_msk"], zero], 1),
        "place": place,
        "b_om": row(np.concatenate([b_off[:, 0], b_off[:, 1], a["b_msk"], zero[0]])),
        "w_out": a["w_out"], "b_out": row(a["b_out"]),
        "affine": np.broadcast_to(np.stack([a["gamma1"], a["ln1_g"], a["ln1_b"], a["gamma2"], a["ln2_g"],
                                            a["ln2_b"]])[None], (128, 6, C)),
        "w_fc1": a["w_fc1"], "b_fc1": row(a["b_fc1"]), "w_fc2": a["w_fc2"], "b_fc2": row(a["b_fc2"]),
        "gate_wt": a["L1_ffn_gate_w"].T, "gate_b": row(a["L1_ffn_gate_b"]),
        "w1": a["L1_ffn_weight1"].reshape(-1, EF), "w2": a["L1_ffn_weight2"].reshape(-1, C),
        "keep": keep,
    }
    nc = _bacc.Bacc("TRN2", target_bir_lowering=False, num_devices=1)
    feeds, args = {}, []
    for name, v in arrays.items():
        v = np.ascontiguousarray(v)
        feeds[f"in_{name}"] = v
        args.append(nc.dram_tensor(f"in_{name}", v.shape, mybir.dt.from_np(v.dtype), kind="ExternalInput").ap())
    args.append(nc.dram_tensor("out_tokens", (NI * L, C), F32, kind="ExternalOutput").ap())
    hybrid(nc, *args)
    r = _run(nc, [feeds], core_ids=[0])
    return r.results[0]["out_tokens"].reshape(NI, HH, WW, C)
```

```python
from contextlib import ExitStack

import numpy as np

import concourse.bass as bass
from concourse import mybir

ALU = mybir.AluOpType
ACT = mybir.ActivationFunctionType
AX = mybir.AxisListType
F32 = mybir.dt.float32
I32 = mybir.dt.int32

NI, HH, WW, C = 8, 56, 56, 128
GR, PT = 4, 9
CG = C // GR
GP = GR * PT
L = HH * WW
TT = 128
NT = -(-L // TT)
LP = NT * TT
TAIL = L - (NT - 1) * TT
RS = 3
NR = 20
WP = WW + 2
HP = RS * NR
PX, PY = WP - 1, RS * NR
TMAX = WP - 1.0
XR = 6 * WP // 3
NE, FF, EF = 64, 512, 512
KT = 4
NG = -(-NT // KT)
SHIFT = 64.0
EPS = 1e-5
RG = 5
NC_OUT = NT // RG

(M_XB, M_MUL, M_Y, M_YT, M_ST1, M_AG1, M_Z1, M_ZA1, M_X1, M_X1T, M_X1B, M_ST2, M_AG2, M_Z2,
 M_ZA2, M_T, M_ST3, M_AG3, M_RSM, M_ZN, M_V, M_ZT) = range(1, 23)
M_N = 22
P_YT, P_OUT, P_X1T, P_FC1, P_FC2, P_ZT = range(1, 7)
P_N = 6
(F_RC, F_T2, F_ST, F_AG, F_Z2) = range(1, 6)
F_N = 5
(I_CC, I_MX, I_SUB, I_RI, I_RF, I_GT, I_FL, I_FM, I_FR, I_OM, I_TI, I_IDX, I_SM, I_RC, I_MK, I_WY,
 I_W) = range(1, 18)
I_N = 17
R_M8, R_NM, R_MR, R_RC, R_MP = range(1, 6)
R_N = 5
LOW = -3.0e38
NL = NT + 1
HP2 = GP // 2
NW = 4


class Step:

    def __init__(self, m, par, u, k):
        self.m, self.par, self.u, self.k = m, par, u, k
        self.n = m * 2 + par
        self.t = u * 2 + k
        self.slot = (par + k) % 2

    def tile(self, ahead=0):
        return self.m * (2 * NT) + self.u * 2 + (NT * (self.par + ahead) + self.k)

    def rows(self, ahead=0):
        return self.m * (2 * NR) + self.u * 2 + (NR * (self.par + ahead) + self.k)

    def gathers(self, last):
        per_pair = NT * GP - (GP - HP2)
        tiles = (NT * self.par + self.k) // 2 + 1
        lasts = (self.par > self.slot) + last
        return self.m * per_pair + self.u * GP + (tiles * GP - lasts * (GP - HP2))


def walk(eng, step, image_end, pool_image, rows_placed=None, two_placed=None, before_last=None):

    def phase(m, par, A, B, D, P):
        with eng.Fori(0, NR // 2) as u:
            for k in range(2):
                step(Step(m, par, u, k), A, B, D, A, False)
        if P:
            pool_image(Step(m, par, NR // 2, 0))
        with eng.Fori(NR // 2, NT // 2) as u:
            for k in range(2):
                step(Step(m, par, u, k), A, B, D, False, False)
        s = Step(m, par, NT // 2, 0)
        step(s, A, B, D, False, True)
        if D:
            image_end(s)

    with eng.Fori(0, NR // 2) as u:
        for k in range(2):
            step(Step(-1, 1, u, k), False, False, False, True, False)
    if rows_placed:
        rows_placed()
    for k in range(2):
        step(Step(-1, 1, 0, k), True, False, False, False, False)
    if two_placed:
        two_placed()
    with eng.Fori(1, NT // 2) as u:
        for k in range(2):
            step(Step(-1, 1, u, k), True, False, False, False, False)
    step(Step(-1, 1, NT // 2, 0), True, False, False, False, True)
    phase(0, 0, True, True, False, False)
    phase(0, 1, True, True, True, False)
    with eng.Fori(1, NI // 2 - 1) as m:
        phase(m, 0, True, True, True, True)
        phase(m, 1, True, True, True, True)
    phase(NI // 2 - 1, 0, True, True, True, True)
    phase(NI // 2 - 1, 1, False, True, True, True)
    if before_last:
        before_last()
    phase(NI // 2, 0, False, False, True, True)
    pool_image(Step(NI // 2, 1, 0, 0))


def hybrid(nc, xpad, xtok, padmask, coords, w_in, b_in, taps, chan, w_om, place, b_om, w_out, b_out, affine,
           w_fc1, b_fc1, w_fc2, b_fc2, gate_wt, gate_b, w1, b1, w2, keep, out):
    ctx = ExitStack()
    with ctx:
        def sb(name, shape, dt=F32):
            return ctx.enter_context(nc.sbuf_tensor(name, shape, dt))

        def psum(name):
            return ctx.enter_context(nc.psum_tensor(name, [128, 512], F32))

        def sem(name):
            return ctx.enter_context(nc.semaphore(name))

        table = [nc.dram_tensor(f"table{b}", [GR * PX * PY, 4 * CG], F32).ap() for b in range(2)]
        t_dram = nc.dram_tensor("t_dram", [NI * LP, C], F32).ap()
        t2_dram = nc.dram_tensor("t2_dram", [NI * LP, C], F32).ap()
        z2_dram = nc.dram_tensor("z2_dram", [NI * LP, C], F32).ap()
        eo_dram = nc.dram_tensor("eo_dram", [NI * NE, C], F32).ap()
        mp_dram = nc.dram_tensor("mp_dram", [NI * NC_OUT * NE, RG * TT], F32).ap()
        table_v = [t.rearrange("(g x y) c -> x g (y c)", g=GR, x=PX) for t in table]

        ident = sb("ident", [128, 128])
        ones = sb("ones", [1, 128])
        nshift = sb("nshift", [128, 1])
        w_in_s = sb("w_in_s", [C, C])
        b_in_s = sb("b_in_s", [1, C])
        taps_s = sb("taps_s", [C, PT])
        chan_s = sb("chan_s", [C, 5])
        bn = sb("bn", [C, 4])
        w_om_s = sb("w_om_s", [C, 4 * GP])
        place_s = sb("place_s", [3, 4 * GP])
        b_om_s = sb("b_om_s", [1, 4 * GP])
        w_out_s = sb("w_out_s", [C, C])
        b_out_s = sb("b_out_s", [1, C])
        aff_s = sb("aff_s", [128, 6, C])
        A1, B1, A2, B2 = (aff_s[:, i, :] for i in (1, 2, 4, 5))
        w_fc1_s = sb("w_fc1_s", [C, FF])
        b_fc1_s = sb("b_fc1_s", [1, FF])
        w_fc2_s = sb("w_fc2_s", [128, FF // 128, C])
        b_fc2_s = sb("b_fc2_s", [1, C])
        gate_w_s = sb("gate_w_s", [C, NE])
        gate_b_s = sb("gate_b_s", [1, NE])
        keep_s = sb("keep_s", [128, NT])

        xrow = sb("xrow", [XR, 2, 3, C])
        prow = sb("prow", [1, 2, 4 * WP])
        xT = sb("xT", [C, 6, WP])
        patch = sb("patch", [PX, GR, RS, 2, 2, CG])
        acc = sb("acc", [C, RS, WW])
        hT = sb("hT", [C, NR * RS * WW])
        co = sb("co", [3, 2, TT])
        hTs = sb("hTs", [C, TT])
        cc = sb("cc", [128, 2 * GP])
        ri = sb("ri", [128, 2 * GP], I32)
        rf = sb("rf", [128, 2 * GP])
        gt = sb("gt", [128, 2 * GP])
        fl = sb("fl", [128, 2 * GP])
        frac = sb("frac", [128, 2 * GP, 2])
        ti = sb("ti", [128, GP])
        sm = sb("sm", [128, 3, GR])
        ex = sb("ex", [128, GP])
        mk = sb("mk", [128, GP])
        wy = sb("wy", [128, GP, 2])
        idx = sb("idx", [128, NT + 2, GP], I32)
        wts = sb("wts", [128, NT, GP, 2, 2])
        idx_now = sb("idx_now", [128, 2, GP], I32)
        gat = sb("gat", [128, 2, GP, 4, CG])
        xt = sb("xt", [128, C])
        xb = sb("xb", [128, C])
        y = sb("y", [128, C])
        yT = sb("yT", [128, TT])
        st = sb("st", [128, 6])
        mv = sb("mv", [128, 2])
        rstd = sb("rstd", [128, 1])
        lnv = sb("lnv", [128, 2])
        eps = sb("eps", [128, 1])
        rstm = sb("rstm", [128, 1])
        z = sb("z", [128, C])
        za = sb("za", [128, C])
        x1 = sb("x1", [128, C])
        x1b = sb("x1b", [128, C])
        x1T = sb("x1T", [128, TT])
        hs = sb("hs", [128, FF])
        tb = sb("tb", [128, C])
        zn = sb("zn", [128, C])
        zT = sb("zT", [C, 2, LP])
        V1 = sb("V1", [128, 2, NT, C + 1])
        E = sb("E", [128, 2, KT * TT])
        tl = sb("tl", [128, C])
        rc = sb("rc", [128, 1])
        t2 = sb("t2", [128, C])
        st2 = sb("st2", [128, 6])
        mv2 = sb("mv2", [128, 2])
        rs2 = sb("rs2", [128, 1])
        z2 = sb("z2", [128, C])
        z2T = sb("z2T", [C, TT])
        probs = sb("probs", [NE, NL * TT])
        picked = sb("picked", [NE, LP])
        rt = sb("rt", [NE, 3])
        top8 = sb("top8", [NE, 8])
        zc = sb("zc", [128, 2, RG, C])
        mpT = sb("mpT", [128, 2, RG, NE])
        pr = sb("pr", [NE, C])
        pooled = sb("pooled", [C, NI, NE])
        b1_s = sb("b1_s", [128, EF // 128, NE])
        ehb = sb("ehb", [128, 2, EF // 128, NI])
        b2_s = sb("b2_s", [NE, C])
        eh = sb("eh", [128, 2, EF // 128, NI])

        ps_s = [psum("ps_s0"), psum("ps_s1")]
        ps_o = psum("ps_o")
        ps_f = psum("ps_f")
        ps_a = psum("ps_a")
        ps_x = [psum("ps_x0"), psum("ps_x1")]
        ps_c = psum("ps_c")

        s_const = sem("s_const")
        s_prep = sem("s_prep")
        s_held = sem("s_held")
        s_bn = sem("s_bn")
        s_prepp = sem("s_prepp")
        s_xrow = sem("s_xrow")
        s_xtr = sem("s_xtr")
        s_xT = sem("s_xT")
        s_xp = sem("s_xp")
        s_patch = sem("s_patch")
        s_pst = sem("s_pst")
        s_patchfree = sem("s_patchfree")
        s_conv9 = sem("s_conv9")
        s_conv = sem("s_conv")
        s_hT = sem("s_hT")
        s_hTs = sem("s_hTs")
        s_co = sem("s_co")
        s_off = sem("s_off")
        s_offfree = sem("s_offfree")
        s_ix = sem("s_ix")
        s_ex = sem("s_ex")
        s_pub = sem("s_pub")
        s_gat = [sem("s_gat0"), sem("s_gat1")]
        s_xt = sem("s_xt")
        s_mlp = sem("s_mlp")
        s_mlp_pe = sem("s_mlp_pe")
        s_rstd = sem("s_rstd")
        s_rs2 = sem("s_rs2")
        s_gelu = sem("s_gelu")
        s_tst = sem("s_tst")
        s_tfree = sem("s_tfree")
        s_S = sem("s_S")
        s_E = sem("s_E")
        s_PV = sem("s_PV")
        s_tl = sem("s_tl")
        s_fin = sem("s_fin")
        s_z2T = sem("s_z2T")
        s_lg = sem("s_lg")
        s_lgc = sem("s_lgc")
        s_t2st = sem("s_t2st")
        s_t2free = sem("s_t2free")
        s_rt = sem("s_rt")
        s_rex = sem("s_rex")
        s_mpst = sem("s_mpst")
        s_zc = sem("s_zc")
        s_mpT = sem("s_mpT")
        s_mpTc = sem("s_mpTc")
        s_pool = sem("s_pool")
        s_pr = sem("s_pr")
        s_prT = sem("s_prT")
        s_mpsc = sem("s_mpsc")
        s_pooled = sem("s_pooled")
        s_half = sem("s_half")
        s_z2Tc = sem("s_z2Tc")
        s_w = [sem(f"s_w{i}") for i in range(NW)]
        s_eh = sem("s_eh")
        s_ehb = sem("s_ehb")
        s_ehg = sem("s_ehg")
        s_eo = sem("s_eo")
        s_eoc = sem("s_eoc")
        s_er = [sem(f"s_er{i}") for i in range(2)]
        s_eTc = sem("s_eTc")
        s_fl = [sem(f"s_fl{i}") for i in range(NW)]
        s_comb = sem("s_comb")
        s_res = sem("s_res")
        s_outst = [sem(f"s_outst{i}") for i in range(NW)]

        NCONST, PREP = 19, 9
        b2_row = w2.rearrange("(e d) h -> e d h", e=NE)[:, EF, :]
        w1_v = w1.rearrange("(e d) h -> e d h", e=NE)
        w2_v = w2.rearrange("(e d) h -> e d h", e=NE)
        spare = V1[:, 0].rearrange("p t c -> p (t c)")
        w1_s = spare[:, 0:NW * EF].rearrange("p (k h) -> p k h", k=NW)
        er = spare[0:NI, NW * EF:NW * EF + 2 * NW * C].rearrange("p (h k c) -> p h k c", h=2, c=C)
        w2_s = zT[:, 0, 0:NW * EF].rearrange("p (k a c) -> p k a c", k=NW, c=C)
        eo = zT[0:NE, 0, NW * EF:NW * EF + NI * C].rearrange("p (n c) -> p n c", n=NI)
        RC = RG * C
        flat = gat[:].rearrange("p s a b c -> p (s a b c)")
        part = [flat[:, 3 * RC * i:3 * RC * (i + 1)] for i in range(NW)]
        t2c = [f[:, 0:RC].rearrange("p (a c) -> p a c", a=RG) for f in part]
        res = [f[:, RC:2 * RC].rearrange("p (a c) -> p a c", a=RG) for f in part]
        mpc = [f[0:NE, 2 * RC:3 * RC] for f in part]

        def hold(eng):
            eng.sem_inc(s_held, 1)

        block = ctx.enter_context(nc.Block())

        @block.sync
        def _(sp):
            for dst, src in ((w_in_s[:], w_in), (b_in_s[:], b_in), (taps_s[:], taps), (chan_s[:], chan),
                             (w_om_s[:], w_om), (place_s[:], place), (b_om_s[:], b_om), (w_out_s[:], w_out),
                             (b_out_s[:], b_out), (aff_s[:], affine), (w_fc1_s[:], w_fc1), (b_fc1_s[:], b_fc1),
                             (w_fc2_s[:], w_fc2.rearrange("(a p) c -> p a c", p=128)), (b_fc2_s[:], b_fc2),
                             (gate_w_s[:], gate_wt), (gate_b_s[:], gate_b), (keep_s[:], keep),
                             (b1_s[:], b1), (b2_s[:], b2_row)):
                sp.dma_start(dst, src).then_inc(s_const, 16)
            sp.sem_inc(s_mpst, 16)
            sp.sem_inc(s_patchfree, 1)
            sp.sem_inc(s_tfree, 1)
            sp.sem_inc(s_t2free, 1)

            def step(s, A, B, D, rows, last):
                if rows:
                    r = s.rows(1)
                    sp.wait_ge(s_patch, r * 2 + 2)
                    hold(sp)
                    sp.dma_start(table_v[1 - s.par][:, :, bass.ds(s.t * (RS * 4 * CG), RS * 4 * CG)],
                                 patch[:].rearrange("x g k a b c -> x g (k a b c)")).then_inc(s_pst, 16)
                    sp.wait_ge(s_pst, (r + 1) * 16)
                    sp.sem_inc(s_patchfree, 1)
                if B:
                    i = s.tile()
                    sp.wait_ge(s_mlp, i * M_N + M_T)
                    hold(sp)
                    sp.dma_start(t_dram[bass.ds(i * TT, TT), :], tb[:]).then_inc(s_tst, 16)
                    sp.wait_ge(s_tst, (i + 1) * 16)
                    sp.sem_inc(s_tfree, 1)
                if D:
                    i = s.tile(-1)
                    sp.wait_ge(s_fin, (i + 1) * F_N + F_Z2)
                    hold(sp)
                    sp.dma_start(t2_dram[bass.ds(i * TT, TT), :], t2[:]).then_inc(s_t2st, 16)
                    sp.dma_start(z2_dram[bass.ds(i * TT, TT), :], z2[:]).then_inc(s_t2st, 16)
                    sp.wait_ge(s_t2st, (i + 1) * 32)
                    sp.sem_inc(s_t2free, 1)

            def pool_image(s):
                i = s.n - 2
                z2_v = z2_dram.rearrange("(n c a p) d -> n c p a d", n=NI, c=NC_OUT, p=TT)
                for c in range(NC_OUT):
                    if c:
                        sp.wait_ge(s_zc, i * (16 * NC_OUT) + 16 * c)
                        hold(sp)
                    sp.wait_ge(s_pool, i * NC_OUT + c + 1)
                    hold(sp)
                    sp.dma_start(zc[:, c % 2], z2_v[bass.ds(i, 1), c].rearrange("o p a d -> (o p) a d"))\
                        .then_inc(s_zc, 16)

            def image_end(s):
                i = s.n - 1
                mp_v = mp_dram.rearrange("(n c e) l -> n e c l", c=NC_OUT, e=NE)
                sp.wait_ge(s_mpsc, i + 1)
                hold(sp)
                sp.dma_start(mp_v[bass.ds(i, 1)].rearrange("o e c l -> (o e) c l"),
                             picked[:].rearrange("e (c l) -> e c l", c=NC_OUT)).then_inc(s_mpst, 16)

            def load_expert(e, k):
                sp.dma_start(w1_s[:, k, :], w1_v[bass.ds(e, 1), 0:C, :].rearrange("o p h -> (o p) h"))\
                    .then_inc(s_w[k], 16)
                sp.dma_start(w2_s[:, k], w2_v[bass.ds(e, 1), 0:EF, :]
                             .rearrange("o (a p) c -> p (o a) c", p=128)).then_inc(s_w[k], 16)

            def first_experts():
                sp.wait_ge(s_PV, (NI - 1) * NT * NG)
                for k in range(NW):
                    load_expert(k, k)

            walk(sp, step, image_end, pool_image, before_last=first_experts)

            def store_outputs(first, half):
                sp.dma_start(eo_dram.rearrange("(n e) c -> n e c", n=NI)[:, bass.ds(first, NW), :], er[:, half])\
                    .then_inc(s_er[half], 16)

            for k in range(NW):
                sp.wait_ge(s_eoc, k + 3)
                load_expert(NW + k, k)
            store_outputs(0, 0)
            with sp.Fori(0, NE // (2 * NW) - 1) as u:
                for k in range(2 * NW):
                    sp.wait_ge(s_eoc, u * (2 * NW) + (NW + k + 3))
                    hold(sp)
                    load_expert(u * (2 * NW) + (2 * NW + k), k % NW)
                    if k % NW == NW - 1:
                        store_outputs(u * (2 * NW) + (k + 1), 1 - k // NW)
            sp.wait_ge(s_eoc, NE + 2)
            store_outputs(NE - NW, 1)
            for half in range(2):
                sp.wait_ge(s_er[half], 16 * (NE // (2 * NW) + 1))
            sp.dma_start(eo, eo_dram.rearrange("(n e) c -> e n c", n=NI)).then_inc(s_eTc, 16)

            out_v = out.rearrange("(n l) d -> n l d", n=NI)
            with sp.Fori(0, 2) as m:
                for q in range(NW * NC_OUT):
                    n, c, k = m * (NI // 2) + q // NC_OUT, q % NC_OUT, q % NW
                    full = RG if c < NC_OUT - 1 else RG - 1
                    sp.wait_ge(s_res, m * (NW * NC_OUT) + q + 3)
                    hold(sp)
                    sp.dma_start(out_v[bass.ds(n, 1), c * RG * TT:(c * RG + full) * TT, :]
                                 .rearrange("o (a p) d -> p (o a) d", p=TT), res[k][:, 0:full, :])\
                        .then_inc(s_outst[k], 16)
                    if full < RG:
                        sp.dma_start(out_v[bass.ds(n, 1), (NT - 1) * TT:L, :].rearrange("o p d -> (o p) d"),
                                     res[k][0:TAIL, RG - 1, :]).then_inc(s_outst[k], 16)
            for k in range(NW):
                sp.wait_ge(s_outst[k], 2 * 16 * (NC_OUT + 1) + 16)

        @block.gpsimd
        def _(pool):
            pool.memset(ident[:], 0.0).then_inc(s_prepp, 1)
            pool.wait_ge(s_prepp, 1)
            pool.affine_select(out=ident[:], in_=ident[:], compare_op=ALU.not_equal, fill=1.0, base=0,
                               pattern=[[-1, 128]], channel_multiplier=1).then_inc(s_prepp, 1)

            def tile(s, samples):
                k = s.slot
                pool.wait_ge(s_pub, s.tile() + 1)
                hold(pool)
                for j in range(samples):
                    pool.indirect_dma_start(gat[:, k, j].rearrange("p a c -> p (a c)"), None, table[s.par],
                                            bass.IndirectOffsetOnAxis(ap=idx_now[:, k, j:j + 1], axis=0))\
                        .then_inc(s_gat[k], 16)

            with pool.Fori(0, NI // 2) as m:
                for par in range(2):
                    with pool.Fori(0, NT // 2) as u:
                        for k in range(2):
                            tile(Step(m, par, u, k), GP)
                    tile(Step(m, par, NT // 2, 0), HP2)

        @block.tensor
        def _(pe):
            pe.wait_ge(s_const, 16 * NCONST)
            pe.wait_ge(s_prepp, 2)
            pe.wait_ge(s_prep, PREP)

            def row_step(s, A):
                r, i, k = s.rows(1), s.tile(1), s.k
                pe.wait_ge(s_xrow, r * 32 + 32)
                if A:
                    pe.wait_ge(s_offfree, i + 1)
                for j in range(3):
                    last = pe.transpose(ps_a[:, j * XR:(j + 1) * XR], xrow[:, k, j, :], ident[0:XR, 0:XR])
                last.then_inc(s_xtr, 1)
                pe.wait_ge(s_xT, r + 1)
                for h in range(2):
                    for j in range(2):
                        for dx in range(2):
                            row = 2 * h + j
                            o = ps_x[h][0:PX, (2 * j + dx) * C:(2 * j + dx + 1) * C]
                            pe.matmul(o, xT[:, row, dx:dx + PX], w_in_s[:], start=True, stop=False)
                            last = pe.matmul(o, prow[0:1, k, row * WP + dx:row * WP + dx + PX], b_in_s[:],
                                             start=False, stop=True)
                    last.then_inc(s_xp, 1)

            def offsets(s, rows):
                i = s.tile(1)
                pe.wait_ge(s_hTs, i + 1)
                pe.wait_ge(s_co, i * 16 + 16)
                if not rows:
                    pe.wait_ge(s_offfree, i + 1)
                o = ps_a[:, 3 * XR:3 * XR + 4 * GP]
                pe.matmul(o, hTs[:], w_om_s[:], start=True, stop=False)
                pe.matmul(o, co[:, s.slot ^ 1, :], place_s[:], start=False, stop=True).then_inc(s_off, 1)

            def scores(s, g):
                b, i = 1 - s.par, s.tile(-1)
                if g >= 2:
                    pe.wait_ge(s_E, i * NG + g - 1)
                for j in range(g * KT, min(g * KT + KT, NT)):
                    last = pe.matmul(ps_s[g % 2][:, (j % KT) * TT:(j % KT + 1) * TT],
                                     zT[:, b, j * TT:(j + 1) * TT], zT[:, b, bass.ds(s.t * TT, TT)],
                                     start=True, stop=True)
                last.then_inc(s_S, 1)

            def values(s, g):
                b, i = 1 - s.par, s.tile(-1)
                if g == 0:
                    pe.wait_ge(s_fin, i * F_N + F_T2)
                pe.wait_ge(s_E, i * NG + g + 1)
                for j in range(g * KT, min(g * KT + KT, NT)):
                    last = pe.matmul(ps_o[:, 0:C + 1], E[:, g % 2, (j % KT) * TT:(j % KT + 1) * TT],
                                     V1[:, b, j, :], start=(j == 0), stop=(j == NT - 1))
                last.then_inc(s_PV, 1)

            def project(s):
                i, q = s.tile(), ps_c
                pe.wait_ge(s_mlp, i * M_N + M_YT)
                pe.matmul(q[:, TT:TT + C], yT[:], w_out_s[:], start=True, stop=False)
                pe.matmul(q[:, TT:TT + C], ones[:], b_out_s[:], start=False, stop=True).then_inc(s_mlp_pe, 1)

            def transpose(s, src, at, after):
                pe.wait_ge(s_mlp, s.tile() * M_N + after)
                pe.transpose(ps_c[:, at * TT:(at + 1) * TT], src[:], ident[:]).then_inc(s_mlp_pe, 1)

            def mlp_in(s):
                pe.wait_ge(s_mlp, s.tile() * M_N + M_X1T)
                for f in range(FF // 128):
                    o = ps_c[:, f * TT:(f + 1) * TT]
                    pe.matmul(o, w_fc1_s[:, f * 128:(f + 1) * 128], x1T[:], start=True, stop=False)
                    last = pe.matmul(o, b_fc1_s[:, f * 128:(f + 1) * 128], ones[:], start=False, stop=True)
                last.then_inc(s_mlp_pe, 1)

            def mlp_out(s):
                pe.wait_ge(s_gelu, s.tile() + 1)
                q = ps_c[:, 0:C]
                for f in range(FF // 128):
                    pe.matmul(q, hs[:, f * TT:(f + 1) * TT], w_fc2_s[:, f, :], start=(f == 0), stop=False)
                pe.matmul(q, ones[:], b_fc2_s[:], start=False, stop=True).then_inc(s_mlp_pe, 1)

            def router_logits(i, j):
                pe.wait_ge(s_fin, i * F_N + F_Z2)
                pe.wait_ge(s_lgc, j + 1)
                pe.transpose(ps_f[:, 0:TT], z2[:], ident[:]).then_inc(s_z2T, 1)
                pe.wait_ge(s_z2Tc, j + 1)
                o = ps_f[0:NE, TT:2 * TT]
                pe.matmul(o, gate_w_s[:], z2T[:], start=True, stop=False)
                pe.matmul(o, gate_b_s[:], ones[:], start=False, stop=True).then_inc(s_lg, 1)

            def step(s, A, B, D, rows, last):
                if D:
                    pe.wait_ge(s_mlp, s.m * (2 * NT * M_N) + s.par * NT * M_N)
                    scores(s, 0)
                if rows:
                    row_step(s, A)
                if D:
                    scores(s, 1)
                    values(s, 0)
                    scores(s, 2)
                    values(s, 1)
                    router_logits(s.tile(-1), (s.n - 1) * NL + s.t)
                if B:
                    transpose(s, y, 0, M_Y)
                if D:
                    scores(s, 3)
                    values(s, 2)
                if B:
                    project(s)
                if D:
                    scores(s, 4)
                    values(s, 3)
                    scores(s, 5)
                    values(s, 4)
                if B:
                    transpose(s, x1, 2, M_X1)
                if D:
                    scores(s, 6)
                    values(s, 5)
                if B:
                    mlp_in(s)
                if D:
                    values(s, 6)
                if B:
                    mlp_out(s)
                if A:
                    offsets(s, rows)
                if B:
                    transpose(s, zn, 1, M_ZN)

            def image_end(s):
                n = s.n - 1
                router_logits(n * NT + NT, n * NL + NT)

            def pool_image(s):
                n = s.n - 2
                pe.wait_ge(s_mpsc, n + 1)
                pe.wait_ge(s_fin, s.tile(-1) * F_N + F_T2)
                hold(pe)

                def transposed(c):
                    if c >= 2:
                        pe.wait_ge(s_mpTc, n * NC_OUT + c - 1)
                        hold(pe)
                    for a in range(RG):
                        j = c * RG + a
                        last = pe.transpose(ps_s[c % 2][:, a * NE:(a + 1) * NE], picked[:, j * TT:(j + 1) * TT],
                                            ident[0:NE, 0:NE])
                    last.then_inc(s_mpT, 1)

                transposed(0)
                for c in range(NC_OUT):
                    if c + 1 < NC_OUT:
                        transposed(c + 1)
                    pe.wait_ge(s_mpTc, n * NC_OUT + c + 1)
                    pe.wait_ge(s_zc, n * (16 * NC_OUT) + 16 * (c + 1))
                    hold(pe)
                    for a in range(RG):
                        last = pe.matmul(ps_o[0:NE, 0:C], mpT[:, c % 2, a, :], zc[:, c % 2, a, :],
                                         start=(c == 0 and a == 0), stop=(c == NC_OUT - 1 and a == RG - 1))
                    last.then_inc(s_pool, 1)
                pe.wait_ge(s_pr, n + 1)
                hold(pe)
                pe.transpose(ps_s[0][:, 0:NE], pr[:], ident[0:NE, 0:NE]).then_inc(s_prT, 1)
                pe.wait_ge(s_pooled, n + 1)
                hold(pe)

            walk(pe, step, image_end, pool_image)

            def hidden(e, u, k):
                pe.wait_ge(s_w[k], u * 32 + 32)
                pe.wait_ge(s_ehb, e + 1)
                for f in range(EF // 128):
                    last = pe.matmul(ps_s[k % 2][:, f * NI:(f + 1) * NI], w1_s[:, k, f * 128:(f + 1) * 128],
                                     pooled[:, :, bass.ds(e, 1)], start=True, stop=True)
                last.then_inc(s_eh, 1)

            def output(e, k):
                pe.wait_ge(s_ehg, e + 1)
                pe.wait_ge(s_eoc, e + 1)
                for f in range(EF // 128):
                    last = pe.matmul((ps_o, ps_f)[k % 2][0:NI, 0:C], eh[:, k % 2, f, :], w2_s[:, k, f, :],
                                     start=(f == 0), stop=(f == EF // 128 - 1))
                last.then_inc(s_eo, 1)

            hidden(0, 0, 0)
            with pe.Fori(0, NE // NW - 1) as u:
                for k in range(NW):
                    hidden(u * NW + k + 1, u + (k + 1) // NW, (k + 1) % NW)
                    output(u * NW + k, k)
            for k in range(NW):
                if k + 1 < NW:
                    hidden(NE - NW + k + 1, NE // NW - 1, k + 1)
                output(NE - NW + k, k)
            pe.wait_ge(s_eTc, 17)
            with pe.Fori(0, 2) as m:
                for q in range(NW * NC_OUT):
                    v, k = m * (NW * NC_OUT) + q, q % NW
                    pe.wait_ge(s_fl[k], m * (32 * NC_OUT) + 32 * (q // NW + 1))
                    pe.wait_ge(s_res, v + 1)
                    hold(pe)
                    for a in range(RG):
                        o = (ps_s if q % 2 else ps_x)[a // 4][:, (a % 4) * C:(a % 4 + 1) * C]
                        last = pe.matmul(o, mpc[k][:, a * TT:(a + 1) * TT],
                                         eo[:, bass.ds(m * (NI // 2) + q // NC_OUT, 1), :]
                                         .rearrange("e o c -> e (o c)"), start=True, stop=True)
                    last.then_inc(s_comb, 1)

        @block.scalar
        def _(act):
            def load_rows(r, k):
                act.dma_start(xrow[:, k], xpad[bass.ds(r * (RS * WP), 3 * XR), :]
                              .rearrange("(k p) c -> p k c", p=XR)).then_inc(s_xrow, 16)
                act.dma_start(prow[0:1, k, :], padmask[0:1, bass.ds(r * (RS * WP), 4 * WP)]).then_inc(s_xrow, 16)

            def load_coords(i, k):
                act.dma_start(co[:, k, :], coords[:, bass.ds(i * TT, TT)]).then_inc(s_co, 16)

            def load_residual(i):
                act.dma_start(xt[:], xtok[bass.ds(i * TT, TT), :]).then_inc(s_xt, 16)

            load_residual(0)
            load_rows(0, 0)
            load_coords(0, 0)
            def root(mean_var, r, tmp, s_own, at):
                act.activation(tmp, mean_var[:, 1:2], ACT.Ln, bias=eps[:, 0:1]).then_inc(s_own, 1)
                act.wait_ge(s_own, at + 1)
                act.activation(r, tmp, ACT.Exp, scale=-0.5).then_inc(s_own, 1)

            act.wait_ge(s_const, 16 * NCONST)
            act.wait_ge(s_prep, 4)
            root(chan_s[:, 3:5], bn[:, 3:4], bn[:, 2:3], s_bn, 0)
            act.wait_ge(s_prep, PREP)

            def step(s, A, B, D, rows, last):
                r, ia = s.rows(1), s.tile(1)
                if rows:
                    act.wait_ge(s_xrow, r * 32 + 32)
                    load_rows(r + 1, 1 - s.k)
                if A:
                    act.wait_ge(s_co, ia * 16 + 16)
                    load_coords(ia + 1, s.slot)
                if D:
                    act.wait_ge(s_tfree, s.m * (2 * NT) + NT * s.par + 1)
                    act.dma_start(tl[:], t_dram[bass.ds(s.tile(-1) * TT, TT), :]).then_inc(s_tl, 16)
                if D:
                    exps(s, 0)
                if rows:
                    act.wait_ge(s_xtr, r + 1)
                    act.copy(xT[:].rearrange("p a b -> p (a b)"), ps_a[:, 0:3 * XR]).then_inc(s_xT, 1)
                    act.wait_ge(s_patchfree, r + 1)
                    for row in range(4):
                        if row % 2 == 0:
                            act.wait_ge(s_xp, r * 2 + row // 2 + 1)
                        src = ps_x[row // 2][0:PX, (row % 2) * 2 * C:(row % 2 + 1) * 2 * C]\
                            .rearrange("p (d g c) -> p d g c", d=2, g=GR)
                        for kk, dy in ((row, 0), (row - 1, 1)):
                            if 0 <= kk < RS:
                                end = act.copy(patch[:, :, kk, :, dy, :].rearrange("p g d c -> p d g c"), src)
                        if row % 2:
                            end.then_inc(s_patch, 1)
                if D:
                    exps(s, 1)
                    exps(s, 2)
                    logits_out((s.n - 1) * NL + s.t, s.t)
                    exps(s, 3)
                if B:
                    i = s.tile()
                    act.wait_ge(s_mlp, i * M_N + M_AG1)
                    load_residual(i + 1)
                    root(mv, rstd[:], lnv[:, 0:1], s_rstd, i * 6)
                if D:
                    for g in range(4, NG):
                        exps(s, g)
                if B:
                    act.preload_act_table_set("gelu_and_others")
                    act.wait_ge(s_mlp_pe, i * P_N + P_FC1)
                    act.activation(hs[:], ps_c[:], ACT.Gelu).then_inc(s_gelu, 1)
                if rows:
                    act.wait_ge(s_conv, r + 1)
                    act.activation(hT[:, bass.ds(s.t * (RS * WW), RS * WW)], acc[:].rearrange("p a b -> p (a b)"),
                                   ACT.Gelu, bias=bn[:, 1:2], scale=bn[:, 0:1]).then_inc(s_hT, 1)
                if A:
                    if rows:
                        act.wait_ge(s_hT, r + 1)
                    act.copy(hTs[:], hT[:, bass.ds(s.t * TT, TT)]).then_inc(s_hTs, 1)
                if B:
                    act.preload_act_table_set("natural_log_exp_and_others")
                if D:
                    act.wait_ge(s_fin, (s.tile(-1) + 1) * F_N + F_AG)
                    root(mv2, rs2[:], lnv[:, 1:2], s_rs2, s.tile(-1) * 2)
                if B:
                    act.wait_ge(s_mlp, i * M_N + M_AG2)
                    root(mv, rstd[:], lnv[:, 0:1], s_rstd, i * 6 + 2)
                if A:
                    act.wait_ge(s_ix, ia * I_N + I_SUB)
                    act.activation(ex[:], ex[:], ACT.Exp).then_inc(s_ex, 1)
                if B:
                    act.wait_ge(s_mlp, i * M_N + M_AG3)
                    root(mv, rstd[:], lnv[:, 0:1], s_rstd, i * 6 + 4)

            def exps(s, g):
                i = s.tile(-1)
                w = min(KT, NT - g * KT) * TT
                act.wait_ge(s_S, i * NG + g + 1)
                if g >= 2:
                    act.wait_ge(s_PV, i * NG + g - 1)
                act.activation(E[:, g % 2, 0:w], ps_s[g % 2][:, 0:w], ACT.Exp, bias=nshift[:, 0:1])\
                    .then_inc(s_E, 1)

            def logits_out(j, t):
                act.wait_ge(s_lg, j + 1)
                act.copy(probs[:, bass.ds(t * TT, TT)], ps_f[0:NE, TT:2 * TT]).then_inc(s_lgc, 1)

            def image_end(s):
                n = s.n - 1
                logits_out(n * NL + NT, NT)
                act.wait_ge(s_rt, n * R_N + R_MR)
                act.activation(probs[:, TT:TT + L], probs[:, TT:TT + L], ACT.Exp, bias=rt[:, 0:1],
                               accum_out=rt[:, 1:2]).then_inc(s_rex, 1)
                act.wait_ge(s_rt, n * R_N + R_MP)
                act.activation(picked[:, 0:L], picked[:, 0:L], ACT.Copy, scale=rt[:, 2:3]).then_inc(s_mpsc, 1)

            def pool_image(s):
                n = s.n - 2
                for c in range(NC_OUT):
                    act.wait_ge(s_mpT, n * NC_OUT + c + 2)
                    act.copy(mpT[:, c % 2].rearrange("p a e -> p (a e)"), ps_s[c % 2][:, 0:RG * NE])\
                        .then_inc(s_mpTc, 1)
                act.wait_ge(s_pool, n * NC_OUT + NC_OUT + 2)
                act.copy(pr[:], ps_o[0:NE, 0:C]).then_inc(s_pr, 1)
                act.wait_ge(s_prT, n + 1)
                act.copy(pooled[:, bass.ds(n, 1), :], ps_s[0][:, 0:NE].unsqueeze(1)).then_inc(s_pooled, 1)

            act.sem_inc(s_lgc, 1)
            act.preload_act_table_set("gelu_and_others")
            walk(act, step, image_end, pool_image,
                 rows_placed=lambda: act.preload_act_table_set("natural_log_exp_and_others"))

            act.preload_act_table_set("gelu_and_others")
            with act.Fori(0, NE // 2) as u:
                for k in range(2):
                    e = u * 2 + k
                    act.wait_ge(s_ehb, e + 2)
                    act.wait_ge(s_eo, e + 1)
                    act.activation(eh[:, k].rearrange("p a n -> p (a n)"), ehb[:, k].rearrange("p a n -> p (a n)"),
                                   ACT.Gelu).then_inc(s_ehg, 1)

            t2_v = t2_dram.rearrange("(q a p) d -> q p a d", a=RG, p=TT)
            mp_v = mp_dram.rearrange("(q e) l -> q e l", e=NE)
            act.wait_ge(s_mpst, 16 * NI + 16)

            def load(q, k):
                act.dma_start(t2c[k], t2_v[bass.ds(q, 1)].rearrange("o p a d -> (o p) a d")).then_inc(s_fl[k], 16)
                act.dma_start(mpc[k], mp_v[bass.ds(q, 1)].rearrange("o e l -> (o e) l")).then_inc(s_fl[k], 16)

            for q in range(NW):
                load(q, q)
            with act.Fori(1, NI * NC_OUT // NW) as u:
                for k in range(NW):
                    act.wait_ge(s_res, u * NW + (k + 3 - NW))
                    hold(act)
                    load(u * NW + k, k)
            act.wait_ge(s_xrow, 32 * (NI * NR + 1))
            act.wait_ge(s_co, 16 * (NI * NT + 1))
            act.wait_ge(s_xt, 16 * (NI * NT + 1))
            for k in range(NW):
                act.wait_ge(s_fl[k], 32 * 2 * NC_OUT)

        @block.vector
        def _(v):
            v.memset(ones[:], 1.0).then_inc(s_prep, 1)
            v.memset(nshift[:], -SHIFT).then_inc(s_prep, 1)
            v.memset(z2[:], 0.0)
            v.memset(picked[:, L:LP], 0.0).then_inc(s_prep, 1)
            v.wait_ge(s_const, 16 * NCONST)
            v.memset(eps[:], EPS).then_inc(s_prep, 1)
            v.wait_ge(s_bn, 2)
            v.tensor_tensor(bn[:, 0:1], bn[:, 3:4], chan_s[:, 1:2], ALU.mult)
            v.tensor_tensor(bn[:, 2:3], chan_s[:, 0:1], chan_s[:, 3:4], ALU.subtract).then_inc(s_prep, 1)
            v.wait_ge(s_prep, 5)
            v.scalar_tensor_tensor(out=bn[:, 1:2], in0=bn[:, 2:3], scalar=bn[:, 0:1], in1=chan_s[:, 2:3],
                                   op0=ALU.mult, op1=ALU.add).then_inc(s_prep, 1)
            v.tensor_tensor(place_s[0:1, :], place_s[0:1, :], b_om_s[:], ALU.add).then_inc(s_prep, 1)
            for b in range(2):
                last = v.tensor_copy(V1[:, b, :, C:C + 1], keep_s[:].unsqueeze(2))
            last.then_inc(s_prep, 1)
            for gamma, rows in ((0, (1, 2)), (3, (4, 5))):
                for i in rows:
                    last = v.tensor_tensor(aff_s[:, i, :], aff_s[:, i, :], aff_s[:, gamma, :], ALU.mult)
            last.then_inc(s_prep, 1)
            v.wait_ge(s_prep, PREP)
            v.sem_inc(s_offfree, 1)
            v.sem_inc(s_eoc, 2)
            v.sem_inc(s_res, 2)
            v.sem_inc(s_er[0], 16)
            v.sem_inc(s_er[1], 16)
            v.sem_inc(s_mpT, 1)
            v.sem_inc(s_pool, 2)
            v.sem_inc(s_ehb, 1)
            v.sem_inc(s_fin, F_N)
            for k in range(NW):
                v.sem_inc(s_outst[k], 16)

            def publish(t, slot):
                v.tensor_copy(idx_now[:, slot, :], idx[:, bass.ds(t, 1), :].rearrange("p o j -> p (o j)"))\
                    .then_inc(s_pub, 1)

            def conv(s, taps):
                r = s.rows(1)
                for tap in taps:
                    src = xT[:, tap // 3:tap // 3 + RS, tap % 3:tap % 3 + WW]
                    if tap == 0:
                        v.wait_ge(s_xT, r + 1)
                        v.tensor_scalar(acc[:], src, taps_s[:, 0:1], None, ALU.mult).then_inc(s_conv9, 1)
                    else:
                        v.wait_ge(s_conv9, r * 8 + tap)
                        v.scalar_tensor_tensor(out=acc[:], in0=src, scalar=taps_s[:, tap:tap + 1], in1=acc[:],
                                               op0=ALU.mult, op1=ALU.add)\
                            .then_inc(s_conv9 if tap < 8 else s_conv, 1)

            def stats_of(src, stats, mean_var, s_own, at):
                v.bn_stats(stats[:], src).then_inc(s_own, 1)
                v.wait_ge(s_own, at + 1)
                hold(v)
                v.bn_aggr(mean_var[:], stats[:]).then_inc(s_own, 1)
                v.wait_ge(s_own, at + 2)

            def sample(s, last):
                i, slot = s.tile(), s.slot
                d, js = i * M_N, (HP2 if last else GP)
                v.wait_ge(s_gat[slot], s.gathers(last) * 16)
                g = gat[:, slot, 0:js].rearrange("p j k c -> p (j k) c")
                w = wts[:, bass.ds(s.t, 1), 0:js].rearrange("p o j a b -> p (o j a b)")
                v.tensor_tensor(g, g, w.unsqueeze(2).to_broadcast([128, 4 * js, CG]), ALU.mult).then_inc(s_mlp, 1)
                v.wait_ge(s_mlp, d + M_MUL)
                total = v.tensor_reduce(y[:, 0:js // PT * CG].rearrange("p (g c) -> p g c", c=CG),
                                        gat[:, slot, 0:js].rearrange("p (g j) k c -> p g c (j k)", j=PT),
                                        AX.X, ALU.add)
                if last:
                    total.then_inc(s_half, 1)
                    v.wait_ge(s_half, (s.n + 1) * 3)
                    v.tensor_copy(y[0:TAIL, C // 2:C], y[TAIL:TT, 0:C // 2]).then_inc(s_mlp, 1)
                else:
                    total.then_inc(s_mlp, 1)

            def block_in(s):
                i = s.tile()
                d, p = i * M_N, i * P_N
                v.wait_ge(s_mlp_pe, p + P_YT)
                v.tensor_copy(yT[:], ps_c[:, 0:TT]).then_inc(s_mlp, 1)
                v.wait_ge(s_mlp_pe, p + P_OUT)
                stats_of(ps_c[:, TT:TT + C], st, mv, s_mlp, d + M_YT)
                v.wait_ge(s_rstd, i * 6 + 2)
                v.tensor_scalar(z[:], ps_c[:, TT:TT + C], mv[:, 0:1], rstd[:, 0:1], ALU.subtract, ALU.mult)\
                    .then_inc(s_mlp, 1)
                v.wait_ge(s_mlp, d + M_Z1)
                v.tensor_tensor(za[:], z[:], A1, ALU.mult).then_inc(s_mlp, 1)
                v.wait_ge(s_mlp, d + M_ZA1)
                v.tensor_tensor(x1[:], za[:], xb[:], ALU.add).then_inc(s_mlp, 1)
                v.wait_ge(s_mlp_pe, p + P_X1T)
                v.tensor_copy(x1T[:], ps_c[:, 2 * TT:3 * TT]).then_inc(s_mlp, 1)
                v.tensor_tensor(x1b[:], x1[:], B2, ALU.add).then_inc(s_mlp, 1)

            def block_stats(s):
                i = s.tile()
                v.wait_ge(s_mlp_pe, i * P_N + P_FC2)
                stats_of(ps_c[:, 0:C], st, mv, s_mlp, i * M_N + M_X1B)

            def block_out(s):
                i = s.tile()
                d = i * M_N
                v.wait_ge(s_rstd, i * 6 + 4)
                v.tensor_scalar(z[:], ps_c[:, 0:C], mv[:, 0:1], rstd[:, 0:1], ALU.subtract, ALU.mult)\
                    .then_inc(s_mlp, 1)
                v.wait_ge(s_mlp, d + M_Z2)
                v.tensor_tensor(za[:], z[:], A2, ALU.mult).then_inc(s_mlp, 1)
                v.wait_ge(s_mlp, d + M_ZA2)
                v.wait_ge(s_tfree, i + 1)
                v.tensor_tensor(tb[:], za[:], x1b[:], ALU.add).then_inc(s_mlp, 1)
                v.wait_ge(s_mlp, d + M_T)
                stats_of(tb[:], st, mv, s_mlp, d + M_T)

            def keys(s):
                i = s.tile()
                d = i * M_N
                v.wait_ge(s_rstd, i * 6 + 6)
                v.tensor_tensor(rstm[:], rstd[:], keep_s[:, bass.ds(s.t, 1)], ALU.mult).then_inc(s_mlp, 1)
                v.wait_ge(s_mlp, d + M_RSM)
                v.tensor_scalar(zn[:], tb[:], mv[:, 0:1], rstm[:, 0:1], ALU.subtract, ALU.mult).then_inc(s_mlp, 1)
                v.wait_ge(s_mlp, d + M_ZN)
                v.tensor_copy(V1[:, s.par, bass.ds(s.t, 1), 0:C], zn[:].unsqueeze(1)).then_inc(s_mlp, 1)

            def keys_transposed(s):
                i = s.tile()
                v.wait_ge(s_mlp_pe, i * P_N + P_ZT)
                v.tensor_copy(zT[:, s.par, bass.ds(s.t * TT, TT)], ps_c[:, TT:2 * TT]).then_inc(s_mlp, 1)

            def attended(s):
                i = s.tile(-1)
                d = (i + 1) * F_N
                v.wait_ge(s_PV, i * NG + NG)
                v.reciprocal(rc[:], ps_o[:, C:C + 1]).then_inc(s_fin, 1)
                v.wait_ge(s_tl, i * 16 + 16)
                v.wait_ge(s_t2free, i + 1)
                v.wait_ge(s_fin, d + F_RC)
                v.scalar_tensor_tensor(out=t2[:], in0=ps_o[:, 0:C], scalar=rc[:, 0:1], in1=tl[:],
                                       op0=ALU.mult, op1=ALU.add).then_inc(s_fin, 1)
                v.wait_ge(s_fin, d + F_T2)
                stats_of(t2[:], st2, mv2, s_fin, d + F_T2)

            def attended_norm(s):
                i = s.tile(-1)
                v.wait_ge(s_rs2, i * 2 + 2)
                v.tensor_scalar(z2[:], t2[:], mv2[:, 0:1], rs2[:, 0:1], ALU.subtract, ALU.mult).then_inc(s_fin, 1)

            def norm_transposed(j):
                v.wait_ge(s_z2T, j + 1)
                v.tensor_copy(z2T[:], ps_f[:, 0:TT]).then_inc(s_z2Tc, 1)

            off = ps_a[:, 3 * XR:3 * XR + 4 * GP]
            lg = off[:, 2 * GP:3 * GP].rearrange("p (g j) -> p g j", g=GR)
            e3 = ex[:].rearrange("p (g j) -> p g j", g=GR)

            def points(s):
                i = s.tile(1)
                d = i * I_N
                v.wait_ge(s_off, i + 1)
                v.tensor_scalar(cc[:], off[:, 0:2 * GP], 0.0, TMAX, ALU.max, ALU.min).then_inc(s_ix, 1)
                v.tensor_reduce(sm[:, 0, :], lg, AX.X, ALU.max).then_inc(s_ix, 1)
                v.wait_ge(s_ix, d + I_MX)
                v.tensor_tensor(e3, lg, sm[:, 0, :].unsqueeze(2).to_broadcast([128, GR, PT]), ALU.subtract)\
                    .then_inc(s_ix, 1)
                v.tensor_copy(ri[:], cc[:]).then_inc(s_ix, 1)
                v.wait_ge(s_ix, d + I_RI)
                v.tensor_copy(rf[:], ri[:]).then_inc(s_ix, 1)
                v.wait_ge(s_ix, d + I_RF)
                v.tensor_tensor(gt[:], rf[:], cc[:], ALU.is_gt).then_inc(s_ix, 1)

            def patch_indices(s, last):
                i = s.tile(1)
                d = i * I_N
                v.wait_ge(s_ix, d + I_GT)
                v.tensor_tensor(fl[:], rf[:], gt[:], ALU.subtract).then_inc(s_ix, 1)
                v.wait_ge(s_ix, d + I_FL)
                v.tensor_scalar(fl[:], fl[:], TMAX - 1.0, None, ALU.min).then_inc(s_ix, 1)
                v.wait_ge(s_ix, d + I_FM)
                v.tensor_tensor(frac[:, :, 1], cc[:], fl[:], ALU.subtract).then_inc(s_ix, 1)
                v.wait_ge(s_ix, d + I_FR)
                v.tensor_scalar(frac[:, :, 0], frac[:, :, 1], -1.0, 1.0, ALU.mult, ALU.add).then_inc(s_ix, 1)
                v.scalar_tensor_tensor(out=ti[:], in0=fl[:, 0:GP], scalar=float(PY), in1=fl[:, GP:2 * GP],
                                       op0=ALU.mult, op1=ALU.add).then_inc(s_ix, 1)
                v.wait_ge(s_ix, d + I_TI)
                at = (s.t + NT - 2) % NT + 2
                v.scalar_tensor_tensor(out=idx[:, bass.ds(at, 1), :].rearrange("p o j -> p (o j)"), in0=ti[:],
                                       scalar=0.25, in1=off[:, 3 * GP:4 * GP], op0=ALU.add, op1=ALU.add)\
                    .then_inc(s_ix, 1)
                v.wait_ge(s_ix, d + I_IDX)
                v.sem_inc(s_offfree, 1)
                if last:
                    v.tensor_copy(idx[TAIL:TT, NT - 1, 0:HP2], idx[0:TAIL, NT - 1, HP2:GP]).then_inc(s_half, 1)

            def corner_weights(s, last):
                i = s.tile(1)
                d = i * I_N
                v.wait_ge(s_ex, i + 1)
                v.tensor_reduce(sm[:, 1, :], e3, AX.X, ALU.add).then_inc(s_ix, 1)
                v.wait_ge(s_ix, d + I_SM)
                v.reciprocal(sm[:, 2, :], sm[:, 1, :]).then_inc(s_ix, 1)
                v.wait_ge(s_ix, d + I_RC)
                v.tensor_tensor(mk[:].rearrange("p (g j) -> p g j", g=GR), e3,
                                sm[:, 2, :].unsqueeze(2).to_broadcast([128, GR, PT]), ALU.mult).then_inc(s_ix, 1)
                v.wait_ge(s_ix, d + I_MK)
                v.tensor_tensor(wy[:], mk[:].unsqueeze(2).to_broadcast([128, GP, 2]), frac[:, GP:2 * GP, :],
                                ALU.mult).then_inc(s_ix, 1)
                v.wait_ge(s_ix, d + I_WY)
                v.tensor_tensor(wts[:, bass.ds(s.t, 1)].rearrange("p o j a b -> p (o j) a b"),
                                frac[:, 0:GP, :].unsqueeze(3).to_broadcast([128, GP, 2, 2]),
                                wy[:].unsqueeze(2).to_broadcast([128, GP, 2, 2]), ALU.mult).then_inc(s_ix, 1)
                if last:
                    v.wait_ge(s_ix, d + I_W)
                    v.tensor_copy(wts[TAIL:TT, NT - 1, 0:HP2], wts[0:TAIL, NT - 1, HP2:GP]).then_inc(s_half, 1)

            def step(s, A, B, D, rows, last):
                if B:
                    v.wait_ge(s_xt, s.tile() * 16 + 16)
                    v.tensor_tensor(xb[:], xt[:], B1, ALU.add).then_inc(s_mlp, 1)
                    sample(s, last)
                    if A and not rows:
                        v.wait_ge(s_patchfree, s.m * (2 * NR) + NR * (s.par + 2) + 1)
                    if A or not last:
                        publish(s.t + 2, s.slot)
                if D:
                    norm_transposed((s.n - 1) * NL + s.t)
                if B:
                    block_in(s)
                if rows:
                    conv(s, range(0, 9))
                if D:
                    attended(s)
                if B:
                    block_stats(s)
                if D:
                    attended_norm(s)
                if A:
                    points(s)
                if B:
                    block_out(s)
                if A:
                    patch_indices(s, last)
                if B:
                    keys(s)
                if A:
                    corner_weights(s, last)
                if B:
                    keys_transposed(s)

            def two_placed():
                v.wait_ge(s_patchfree, NR + 1)
                v.wait_ge(s_ix, 2 * I_N)
                publish(NT, 0)
                publish(NT + 1, 1)

            def image_end(s):
                n = s.n - 1
                d = n * R_N
                p, k = probs[:, TT:TT + L], picked[:, 0:L]
                norm_transposed(n * NL + NT)
                v.wait_ge(s_lgc, n * NL + NL + 1)
                hold(v)
                v.max(top8[:], p).then_inc(s_rt, 1)
                v.wait_ge(s_rt, d + R_M8)
                v.tensor_scalar(rt[:, 0:1], top8[:, 0:1], -1.0, None, ALU.mult).then_inc(s_rt, 1)
                v.wait_ge(s_mpst, n * 16 + 16)
                v.wait_ge(s_mpT, n * NC_OUT + 1)
                hold(v)
                v.match_replace(k, top8[:], p, LOW).then_inc(s_rt, 1)
                v.wait_ge(s_rex, n + 1)
                v.reciprocal(rt[:, 2:3], rt[:, 1:2]).then_inc(s_rt, 1)
                v.wait_ge(s_rt, d + R_MR)
                v.scalar_tensor_tensor(out=k, in0=k, scalar=LOW, in1=p, op0=ALU.is_le, op1=ALU.mult)\
                    .then_inc(s_rt, 1)

            def pool_image(s):
                pass

            walk(v, step, image_end, pool_image, two_placed=two_placed)

            def bias(e, k):
                v.wait_ge(s_eh, e + 1)
                v.tensor_tensor(ehb[:, k], ps_s[k][:, 0:EF // 128 * NI].rearrange("p (a n) -> p a n", n=NI),
                                b1_s[:, :, bass.ds(e, 1)].to_broadcast([128, EF // 128, NI]), ALU.add)\
                    .then_inc(s_ehb, 1)

            def collect(e, u, k):
                half = k // NW
                v.wait_ge(s_eo, e + 2)
                if k % NW == 0:
                    v.wait_ge(s_er[half], u * 16 + 16)
                v.tensor_copy(er[:, half, k % NW, :], (ps_o, ps_f)[k % 2][0:NI, 0:C]).then_inc(s_eoc, 1)

            v.sem_inc(s_eo, 1)
            bias(0, 0)
            with v.Fori(0, NE // (2 * NW) - 1) as u:
                for k in range(2 * NW):
                    bias(u * (2 * NW) + k + 1, (k + 1) % 2)
                    collect(u * (2 * NW) + k, u, k)
            for k in range(2 * NW):
                e = NE - 2 * NW + k
                if e + 1 < NE:
                    bias(e + 1, (k + 1) % 2)
                collect(e, NE // (2 * NW) - 1, k)
            v.wait_ge(s_eTc, 16)
            v.tensor_tensor(eo, eo, b2_s[:].unsqueeze(1).to_broadcast([NE, NI, C]), ALU.add).then_inc(s_eTc, 1)
            with v.Fori(0, 2) as m:
                for q in range(NW * NC_OUT):
                    w, k = m * (NW * NC_OUT) + q, q % NW
                    v.wait_ge(s_comb, w + 1)
                    if q >= NW:
                        done = sum(2 if x % NC_OUT == NC_OUT - 1 else 1 for x in range(q) if x % NW == k)
                    else:
                        done = 0
                    v.wait_ge(s_outst[k], m * (16 * (NC_OUT + 1)) + 16 * done + 16)
                    b = ps_s if q % 2 else ps_x
                    v.tensor_tensor(res[k][:, 0:4, :].rearrange("p a c -> p (a c)"), b[0][:],
                                    t2c[k][:, 0:4, :].rearrange("p a c -> p (a c)"), ALU.add)
                    v.tensor_tensor(res[k][:, 4, :], b[1][:, 0:C], t2c[k][:, 4, :], ALU.add).then_inc(s_res, 1)


def _constants():
    tok = np.arange(LP)
    real = tok < L
    one = np.stack([np.ones(LP), np.where(real, tok % WW + 1, 1), np.where(real, tok // WW + 1, 1)])
    coords = np.concatenate([np.tile(one, (1, NI)), one[:, :TT]], 1).astype(np.float32)
    place = np.zeros((3, 4 * GP), np.float32)
    point = np.tile(np.arange(PT), GR)
    place[0, 0:GP], place[0, GP:2 * GP] = point // 3 - 1, point % 3 - 1
    place[1, 0:GP] = 1
    place[2, GP:2 * GP] = 1
    place[0, 3 * GP:] = np.repeat(np.arange(GR), PT) * (PX * PY)
    mask = np.zeros((NI, HP, WP), np.float32)
    mask[:, 1:HH + 1, 1:WW + 1] = 1
    mask = np.concatenate([mask.reshape(-1), np.zeros(2 * RS * WP, np.float32)])
    keep = (np.arange(TT)[:, None] + np.arange(NT)[None] * TT < L).astype(np.float32)
    return coords, place, mask.reshape(1, -1), keep


def kernel(**inputs):
    import concourse.bacc as _bacc
    from concourse.bass_utils import run_bass_kernel_spmd as _run

    a = {k.removeprefix("L0_conv_"): np.asarray(v) for k, v in inputs.items()}
    x = a["x"]
    coords, place, mask, keep = _constants()
    row = lambda v: v.reshape(1, -1)
    xpad = np.zeros((NI, HP, WP, C), x.dtype)
    xpad[:, 1:HH + 1, 1:WW + 1] = x
    xtok = np.zeros((NI * LP + TT, C), x.dtype)
    xtok[:NI * LP].reshape(NI, LP, C)[:, :L] = x.reshape(NI, L, C)
    w_off, b_off = a["w_off"].reshape(C, GP, 2), a["b_off"].reshape(GP, 2)
    zero = np.zeros((C, GP), x.dtype)
    arrays = {
        "xpad": np.concatenate([xpad.reshape(-1, C), np.zeros((2 * RS * WP, C), x.dtype)]),
        "xtok": xtok,
        "padmask": mask,
        "coords": coords,
        "w_in": a["w_in"], "b_in": row(a["b_in"]),
        "taps": a["dw_w"].reshape(C, PT),
        "chan": np.stack([a["dw_b"], a["bn_g"], a["bn_b"], a["bn_m"], a["bn_v"]], 1),
        "w_om": np.concatenate([w_off[..., 0], w_off[..., 1], a["w_msk"], zero], 1),
        "place": place,
        "b_om": row(np.concatenate([b_off[:, 0], b_off[:, 1], a["b_msk"], zero[0]])),
        "w_out": a["w_out"], "b_out": row(a["b_out"]),
        "affine": np.broadcast_to(np.stack([a["gamma1"], a["ln1_g"], a["ln1_b"], a["gamma2"], a["ln2_g"],
                                            a["ln2_b"]])[None], (128, 6, C)),
        "w_fc1": a["w_fc1"], "b_fc1": row(a["b_fc1"]), "w_fc2": a["w_fc2"], "b_fc2": row(a["b_fc2"]),
        "gate_wt": a["L1_ffn_gate_w"].T, "gate_b": row(a["L1_ffn_gate_b"]),
        "w1": a["L1_ffn_weight1"].reshape(-1, EF),
        "b1": a["L1_ffn_weight1"][:, C, :].reshape(NE, EF // 128, 128).transpose(2, 1, 0),
        "w2": a["L1_ffn_weight2"].reshape(-1, C),
        "keep": keep,
    }
    nc = _bacc.Bacc("TRN2", target_bir_lowering=False, num_devices=1)
    feeds, args = {}, []
    for name, v in arrays.items():
        v = np.ascontiguousarray(v)
        feeds[f"in_{name}"] = v
        args.append(nc.dram_tensor(f"in_{name}", v.shape, mybir.dt.from_np(v.dtype), kind="ExternalInput").ap())
    args.append(nc.dram_tensor("out_tokens", (NI * L, C), F32, kind="ExternalOutput").ap())
    hybrid(nc, *args)
    r = _run(nc, [feeds], core_ids=[0])
    return r.results[0]["out_tokens"].reshape(NI, HH, WW, C)
```
